# Optimizing a Trainium2 kernel written in Bass

```python
import numpy as np
import jax
import jax.numpy as jnp

def _softmax(x, axis=-1):
    return jax.nn.softmax(x, axis=axis)

def _gelu(x):
    return jax.nn.gelu(x, approximate=True)

def _silu(x):
    return jax.nn.silu(x)

def _sigmoid(x):
    return jax.nn.sigmoid(x)

def _layernorm(x, axis=-1, eps=1e-05):
    m = jnp.mean(x, axis=axis, keepdims=True)
    v = jnp.var(x, axis=axis, keepdims=True)
    return (x - m) / jnp.sqrt(v + eps)

def _scatter_add(tgt, idx, src, axis=0):
    return tgt.at[idx].add(src)

def _segment_sum(src, seg, n):
    return jax.ops.segment_sum(src, seg, n)
kernel_name = 'mk_macaron_d1_jaxref_r8_60652c'

def setup_inputs(seed: int=0):
    np.random.seed(seed)
    _w = jnp.asarray

    def _L0_attn_setup():
        import jax, jax.numpy as jnp
        import numpy as np
        B, S, D = (4, 256, 128)
        key = jax.random.key(seed)
        k1, k2, k3, k4 = jax.random.split(key, 4)
        x = jax.random.normal(k1, (B, S, D), dtype=jnp.float32)
        Qw = jax.random.normal(k2, (D, D), dtype=jnp.float32) / 40
        Kw = jax.random.normal(k3, (D, D), dtype=jnp.float32) / 40
        Vw = jax.random.normal(k4, (D, D), dtype=jnp.float32) / 40
        return {'x': x, 'Qw': Qw, 'Kw': Kw, 'Vw': Vw}
    _L0_attn_in = _L0_attn_setup()

    def _L0_ffn_setup():
        import jax, jax.numpy as jnp
        import numpy as np
        B, S, D, H, E = (2, 256, 128, 512, 8)
        key = jax.random.key(seed)
        k0, k1, k2, k3 = jax.random.split(key, 4)
        x = jax.random.normal(k0, (B, S, D), dtype=jnp.float32)
        router_w = jax.random.normal(k1, (E, D), dtype=jnp.float32) * 0.02
        w1 = jax.random.normal(k2, (E, D, H), dtype=jnp.float32) * 0.02
        w2 = jax.random.normal(k3, (E, H, D), dtype=jnp.float32) * 0.02
        return {'x': x, 'router_w': router_w, 'w1': w1, 'w2': w2}
    _L0_ffn_in = _L0_ffn_setup()
    _d = {'L0_attn_x': _L0_attn_in['x'], 'L0_attn_Qw': _L0_attn_in['Qw'], 'L0_attn_Kw': _L0_attn_in['Kw'], 'L0_attn_Vw': _L0_attn_in['Vw'], 'L0_ffn_router_w': _L0_ffn_in['router_w'], 'L0_ffn_w1': _L0_ffn_in['w1'], 'L0_ffn_w2': _L0_ffn_in['w2']}
    _x0 = _d['L0_attn_x']
    _d['L0_attn_x'] = jax.random.normal(jax.random.fold_in(jax.random.key(seed), 1), (4, 512, 128), dtype=_x0.dtype)
    del _x0
    return _d

def reference(L0_attn_x, L0_attn_Qw, L0_attn_Kw, L0_attn_Vw, L0_ffn_router_w, L0_ffn_w1, L0_ffn_w2):

    def _L0_attn_ref(x, Qw, Kw, Vw):
        import jax, jax.numpy as jnp
        import numpy as np
        B, S, D = (4, 256, 128)
        Q = x @ Qw
        K = x @ Kw
        V = x @ Vw
        d = x.shape[-1]
        S_len = x.shape[-2]
        mask = jnp.where(jnp.tril(jnp.ones((S_len, S_len), dtype=x.dtype)) == 0, -jnp.inf, 0.0).astype(x.dtype)
        scores = jnp.einsum('bqd,bkd->bqk', Q, K) / jnp.sqrt(jnp.asarray(d, x.dtype))
        scores = scores + mask
        attn = jax.nn.softmax(scores, axis=-1)
        return jnp.einsum('bqk,bkd->bqd', attn, V)

    def _L0_ffn_ref(x, router_w, w1, w2):
        import jax, jax.numpy as jnp
        import numpy as np
        B, S, D, H, E = (2, 256, 128, 512, 8)
        b, s, d = x.shape
        e = router_w.shape[0]
        xf = x.reshape(-1, d)
        probs = jax.nn.softmax(xf @ router_w.T, axis=-1)
        topv, topi = jax.lax.top_k(probs, 2)
        topv = topv / (topv.sum(axis=-1, keepdims=True) + 1e-09)
        cw = (jax.nn.one_hot(topi, e, dtype=xf.dtype) * topv[..., None]).sum(axis=1)
        h = jax.nn.gelu(jnp.einsum('td,edh->teh', xf, w1), approximate=False)
        y = jnp.einsum('teh,ehd->ted', h, w2)
        out = jnp.einsum('te,ted->td', cw, y)
        return out.reshape(b, s, d)
    x = L0_attn_x
    x = x + 0.5 * _L0_ffn_ref(_layernorm(x, axis=-1), L0_ffn_router_w, L0_ffn_w1, L0_ffn_w2)
    x = x + _L0_attn_ref(_layernorm(x, axis=-1), L0_attn_Qw, L0_attn_Kw, L0_attn_Vw)
    x = x + 0.5 * _L0_ffn_ref(_layernorm(x, axis=-1), L0_ffn_router_w, L0_ffn_w1, L0_ffn_w2)
    return x

_drawn_inputs = setup_inputs


def setup_inputs(seed=0):
    import zlib

    import numpy as np

    out = dict(_drawn_inputs(seed))
    spreads = {}
    factors = {'L0_attn_Qw': 8.0, 'L0_attn_Kw': 8.0}
    for name, (base, spread) in spreads.items():
        noise = np.random.default_rng([zlib.crc32(name.encode()), seed]).standard_normal(out[name].shape)
        drawn = base * np.exp(spread * noise) if base else spread * noise
        out[name] = jnp.asarray(drawn.astype(out[name].dtype))
    for name, factor in factors.items():
        out[name] = (out[name] * factor).astype(out[name].dtype)
    return out
```

```python
from contextlib import ExitStack

import concourse.bass as bass
from concourse import mybir

F32 = mybir.dt.float32
F32R = mybir.dt.float32r
BF16 = mybir.dt.bfloat16
I32 = mybir.dt.int32
ALU = mybir.AluOpType
ACT = mybir.ActivationFunctionType
AX = mybir.AxisListType.X

P = 128
D = 128
H = 512
E = 8
TOP = 2
BATCH, SEQ = 4, 512
TILES = BATCH * SEQ // P
GROUPS = 2
GT = TILES // GROUPS
HALF = GT // 2
HC = H // P
MAX_BLOCKS = (GT * P * TOP + (P - 1) * E) // P
LAG = 3
UNROLL = 4
LOOPS = (MAX_BLOCKS - LAG) // UNROLL
assert LOOPS * UNROLL + LAG == MAX_BLOCKS
LN_EPS = 1e-5
TOPK_EPS = 1e-9
SCORE_SCALE = float(D) ** -0.5
MASKED = -3.0e38
RSQRT_MAGIC = float(0x5F3759DF)
NEWTON_STEPS = 3


def macaron(nc, x, q_w, k_w, v_w, router_w, w1, w2, out):
    with ExitStack() as ctx:
        def sb(name, shape, dt=F32):
            return ctx.enter_context(nc.sbuf_tensor(name, shape, dt))

        def sem(name):
            return ctx.enter_context(nc.semaphore(name))

        slots_in = [nc.dram_tensor(f"slots_in{g}", (MAX_BLOCKS * P, D), F32).ap() for g in range(GROUPS)]
        slots_out = [nc.dram_tensor(f"slots_out{g}", (MAX_BLOCKS * P, D), F32).ap() for g in range(GROUPS)]

        w1_raw, w2_raw = sb("w1_raw", [P, E, H]), sb("w2_raw", [P, E, HC, D])
        w1_hi, w1_lo = sb("w1_hi", [P, E * H], F32R), sb("w1_lo", [P, E * H], F32R)
        w2_hi, w2_lo = sb("w2_hi", [P, E * H], F32R), sb("w2_lo", [P, E * H], F32R)
        qw, kw, vw = sb("qw", [P, D]), sb("kw", [P, D]), sb("vw", [P, D])
        router_rows, router_T = sb("router_rows", [E, D]), sb("router_T", [P, E])
        ident, ident16 = sb("ident", [P, P]), sb("ident16", [P, P], BF16)
        before16 = sb("before16", [P, P], BF16)
        ones16 = sb("ones16", [P, P], BF16)
        causal16 = sb("causal16", [P, P], BF16)
        rev_e = sb("rev_e", [P, E])
        block_floor = sb("block_floor", [P, E, GT])
        block_no = sb("block_no", [1, MAX_BLOCKS, E - 1])
        zeros = sb("zeros", [P, MAX_BLOCKS * D])

        xs = sb("xs", [P, TILES, D])
        xn = [sb(f"xn{g}", [P, GT, D]) for g in range(GROUPS)]
        stats, moments = sb("stats", [P, GT, 6]), sb("moments", [P, GT, 2])
        var_eps, rstd, newton = sb("var_eps", [P, GT]), sb("rstd", [P, GT]), sb("newton", [P, GT])
        half_bits = sb("half_bits", [P, GT], I32)
        nT = sb("nT", [P, 2, HALF * P])

        logit, shifted, expd = sb("logit", [P, GT, E]), sb("shifted", [P, GT, E]), sb("expd", [P, GT, E])
        key, logit2, work = sb("key", [P, GT, E]), sb("logit2", [P, GT, E]), sb("work", [P, GT, E])
        pick1, pick2 = sb("pick1", [P, GT, E]), sb("pick2", [P, GT, E])
        picked16 = sb("picked16", [P, GT, E], BF16)
        top, best = sb("top", [P, GT]), sb("best", [P, GT])
        prob1, prob2, den = sb("prob1", [P, GT]), sb("prob2", [P, GT]), sb("den", [P, GT])
        gate = [sb(f"gate{g}", [P, TOP, GT]) for g in range(GROUPS)]
        over = sb("over", [P, E, GT])
        n_blocks, last_block, first_block = sb("n_blocks", [P, E]), sb("last_block", [P, E]), sb("first_block", [P, E])
        slot = sb("slot", [P, GT, E])
        slot_f = sb("slot_f", [P, TOP, GT])
        slot_of = [sb(f"slot_of{g}", [P, TOP, GT], I32) for g in range(GROUPS)]
        past = sb("past", [1, MAX_BLOCKS, E - 1])
        expert_f = sb("expert_f", [1, MAX_BLOCKS])
        expert_at = [sb(f"expert_at{g}", [1, MAX_BLOCKS], I32) for g in range(GROUPS)]

        xb = [sb(f"xb{k}", [P, D]) for k in range(UNROLL)]
        xT_hi = [sb(f"xT_hi{k}", [P, P], F32R) for k in range(2)]
        xT_lo = [sb(f"xT_lo{k}", [P, P], F32R) for k in range(2)]
        act = [sb(f"act{k}", [P, H]) for k in range(2)]
        aT_hi = [sb(f"aT_hi{k}", [P, H], F32R) for k in range(2)]
        aT_lo = [sb(f"aT_lo{k}", [P, H], F32R) for k in range(2)]
        yb = [sb(f"yb{k}", [P, D]) for k in range(UNROLL)]
        y_rows = [sb(f"y_rows{g}", [P, GT, TOP, D]) for g in range(GROUPS)]

        QT, KT, V = sb("QT", [P, SEQ]), sb("KT", [P, SEQ]), sb("V", [P, HALF, D])
        probs = [sb(f"probs{k}", [P, SEQ]) for k in range(2)]
        probs_T = sb("probs_T", [P, SEQ])
        neg_max, exp_bias = sb("neg_max", [P, TILES]), sb("exp_bias", [P, TILES])
        row_sum, row_inv = sb("row_sum", [P, TILES]), sb("row_inv", [P, TILES])

        bank = [ctx.enter_context(nc.psum_tensor(f"bank{k}", [P, 512], F32)) for k in range(8)]
        xT_ps, h_ps, aT_ps, y_ps = bank[0:2], bank[2:4], bank[4:6], bank[6:8]
        nT_ps = bank[0:2]
        logit_ps, rank_ps, count_ps, router_ps = bank[2], bank[3], bank[4], bank[5]
        q_ps, k_ps, v_ps, s_ps, pT_ps, o_ps = bank[2], bank[3], bank[4], bank[5:7], bank[7], bank[0:2]

        x_in = [sem(f"x_in{g}") for g in range(GROUPS)]
        router_in, attn_w_in, w1_in, w2_in = sem("router_in"), sem("attn_w_in"), sem("w1_in"), sem("w2_in")
        consts, zeros_set, slots_zeroed = sem("consts"), sem("zeros_set"), sem("slots_zeroed")
        router_T_ps, router_T_sb = sem("router_T_ps"), sem("router_T_sb")
        w_hi_done, w_lo_done = sem("w_hi_done"), sem("w_lo_done")
        dve_step = sem("dve_step")
        normed, nT_written, nT_copied, nT_used = sem("normed"), sem("nT_written"), sem("nT_copied"), sem("nT_used")
        shifted_ready, expd_ready = sem("shifted_ready"), sem("expd_ready")
        picked_ready, ranked, routed = sem("picked_ready"), sem("ranked"), sem("routed")
        scattered = [sem(f"scattered{g}") for g in range(GROUPS)]
        gathered = [[sem(f"gathered{g}_{t}") for t in range(GT)] for g in range(GROUPS)]
        x_loaded = [sem(f"x_loaded{k}") for k in range(UNROLL)]
        y_stored = [sem(f"y_stored{k}") for k in range(UNROLL)]
        xT_ready, xhi_ready, xlo_ready = sem("xT_ready"), sem("xhi_ready"), sem("xlo_ready")
        h_ready, act_ready, aT_ready = sem("h_ready"), sem("act_ready"), sem("aT_ready")
        ahi_ready, alo_ready, y_ready, y_copied = sem("ahi_ready"), sem("alo_ready"), sem("y_ready"), sem("y_copied")
        q_written, k_written = sem("q_written"), sem("k_written")
        q_copied, k_copied, v_copied = sem("q_copied"), sem("k_copied"), sem("v_copied")
        scored, bias_ready, exped = sem("scored"), sem("bias_ready"), sem("exped")
        pT_written, pT_copied, o_written, attended = sem("pT_written"), sem("pT_copied"), sem("o_written"), sem("attended")
        combined, out_stored = sem("combined"), sem("out_stored")

        block = ctx.enter_context(nc.Block())

        NORM_OF_ROUTE = [0, 1, 3, 5]
        NORM_OF_ATTEND = [2, 4]

        def group_tiles(g):
            return range(g * GT, (g + 1) * GT)

        def nth(c, i):
            return c + UNROLL * i

        def uses(c, i):
            return c // UNROLL + 1 + i

        def run_steps(eng, p, step):
            base = p * MAX_BLOCKS
            for s in range(LAG):
                step([L for L in range(LAG + 1) if s - L >= 0], base + s, s, 0)
            with eng.Fori(0, LOOPS) as i:
                for j in range(UNROLL):
                    step(list(range(LAG + 1)), base + LAG + j, LAG + j, i)
            for s in range(MAX_BLOCKS, MAX_BLOCKS + LAG):
                step([L for L in range(LAG + 1) if s - L < MAX_BLOCKS], base + s, s, 0)

        @block.sync
        def _(sp):
            x_tiles = x.rearrange("b (t p) d -> p (b t) d", p=P)
            for g in range(GROUPS):
                for h in range(2):
                    t0 = g * GT + h * HALF
                    sp.dma_start(xs[:, t0:t0 + HALF, :], x_tiles[:, t0:t0 + HALF, :]).then_inc(x_in[g], 16)
                if g == 0:
                    sp.dma_start(router_rows[:], router_w).then_inc(router_in, 16)
            for e in range(0, E, 2):
                sp.dma_start(w1_raw[:, e:e + 2, :], w1[e:e + 2].rearrange("e d h -> d e h")).then_inc(w1_in, 16)
            for e in range(0, E, 2):
                sp.dma_start(w2_raw[:, e:e + 2], w2[e:e + 2].rearrange("e (c p) d -> p e c d", p=P)).then_inc(w2_in, 16)
            for dst, src in ((qw, q_w), (kw, k_w), (vw, v_w)):
                sp.dma_start(dst[:], src).then_inc(attn_w_in, 16)

            def load(g, b, c, i):
                k = c % UNROLL
                if c >= UNROLL:
                    sp.wait_ge(xT_ready, nth(c, i) - UNROLL + 1)
                sp.dma_start(xb[k][:], slots_in[g][bass.ds(b * P, P), :]).then_inc(x_loaded[k], 16)

            def store(g, b, c, i):
                k = c % UNROLL
                sp.wait_ge(y_copied, nth(c, i) + 1)
                sp.dma_start(slots_out[g][bass.ds(b * P, P), :], yb[k][:]).then_inc(y_stored[k], 16)

            def expert_phase(p):
                g = p % GROUPS
                base = p * MAX_BLOCKS
                sp.wait_ge(scattered[g], 16 * TOP * GT * (p // GROUPS + 1))
                for b in range(UNROLL):
                    load(g, b, base + b, 0)
                with sp.Fori(0, LOOPS - 1) as i:
                    for j in range(UNROLL):
                        store(g, j + UNROLL * i, base + j, i)
                        load(g, j + UNROLL * (i + 1), base + j + UNROLL, i)
                for b in range(UNROLL * (LOOPS - 1), MAX_BLOCKS):
                    store(g, b, base + b, 0)
                    if b + UNROLL < MAX_BLOCKS:
                        load(g, b + UNROLL, base + b + UNROLL, 0)

            for p in range(2 * GROUPS):
                expert_phase(p)
            o_tiles = out.rearrange("b (t p) d -> p (b t) d", p=P)
            for g in range(GROUPS):
                for h in range(2):
                    t0 = g * GT + h * HALF
                    sp.wait_ge(combined, (GROUPS + g) * GT + (h + 1) * HALF)
                    sp.dma_start(o_tiles[:, t0:t0 + HALF, :], xs[:, t0:t0 + HALF, :]).then_inc(out_stored, 16)
            sp.wait_ge(out_stored, 16 * 2 * GROUPS)

        @block.gpsimd
        def _(pool):
            pool.memset(zeros[:], 0.0).then_inc(zeros_set, 1)
            pool.memset(ident[:], 0.0).then_inc(consts, 1)
            pool.memset(ident16[:], 0.0).then_inc(consts, 1)
            pool.memset(before16[:], 1.0).then_inc(consts, 1)
            pool.memset(ones16[:], 1.0).then_inc(consts, 1)
            pool.memset(causal16[:], 0.0).then_inc(consts, 1)
            pool.wait_ge(consts, 5)
            for m in (ident, ident16):
                pool.affine_select(out=m[:], in_=m[:], compare_op=ALU.not_equal, fill=1.0, base=0,
                                   pattern=[[-1, P]], channel_multiplier=1).then_inc(consts, 1)
            pool.affine_select(out=before16[:], in_=before16[:], compare_op=ALU.is_gt, fill=0.0, base=0,
                               pattern=[[1, P]], channel_multiplier=-1).then_inc(consts, 1)
            pool.affine_select(out=causal16[:], in_=causal16[:], compare_op=ALU.is_ge, fill=MASKED, base=0,
                               pattern=[[-1, P]], channel_multiplier=1).then_inc(consts, 1)
            pool.iota(rev_e[:], [[-1, E]], base=E, channel_multiplier=0,
                      allow_small_or_imprecise_dtypes=True).then_inc(consts, 1)
            pool.iota(block_floor[:], [[0, E], [P, GT]], base=0, channel_multiplier=0,
                      allow_small_or_imprecise_dtypes=True).then_inc(consts, 1)
            pool.iota(block_no[:], [[1, MAX_BLOCKS], [0, E - 1]], base=0, channel_multiplier=0,
                      allow_small_or_imprecise_dtypes=True).then_inc(consts, 1)
            pool.wait_ge(zeros_set, 1)
            for g in range(GROUPS):
                pool.dma_start(slots_in[g].rearrange("(p n) d -> p (n d)", p=P), zeros[:]).then_inc(slots_zeroed, 16)
            pool.wait_ge(slots_zeroed, 16 * GROUPS)

            def scatter(r):
                g = r % GROUPS
                pool.wait_ge(routed, r + 1)
                for t in range(GT):
                    for k in range(TOP):
                        pool.indirect_dma_start(
                            slots_in[g], bass.IndirectOffsetOnAxis(ap=slot_of[g][:, k, t:t + 1], axis=0),
                            xn[g][:, t, :], None).then_inc(scattered[g], 16)

            def gather(p):
                g = p % GROUPS
                for k in range(UNROLL):
                    done = len([G for G in range((p + 1) * MAX_BLOCKS) if G % UNROLL == k])
                    pool.wait_ge(y_stored[k], 16 * done)
                for t in range(GT):
                    for k in range(TOP):
                        pool.indirect_dma_start(
                            y_rows[g][:, t, k, :], None, slots_out[g],
                            bass.IndirectOffsetOnAxis(ap=slot_of[g][:, k, t:t + 1], axis=0)
                        ).then_inc(gathered[g][t], 16)

            scatter(0)
            scatter(1)
            gather(0)
            gather(1)
            scatter(2)
            scatter(3)
            gather(2)
            gather(3)

        @block.scalar
        def _(sc):
            def copy_nT(n, h):
                idx = 2 * n + h
                sc.wait_ge(nT_written, idx + 1)
                if idx >= 2:
                    sc.wait_ge(nT_used, idx - 1)
                nc.scalar.copy(nT[:, h, :], nT_ps[h][:]).then_inc(nT_copied, 1)

            def route(r):
                for h in range(2):
                    copy_nT(NORM_OF_ROUTE[r], h)
                sc.wait_ge(shifted_ready, r + 1)
                nc.scalar.activation(expd[:], shifted[:], ACT.Exp).then_inc(expd_ready, 1)

            def split_weights():
                for src, dst, arrived in ((w1_raw[:].rearrange("p e h -> p (e h)"), w1_hi, w1_in),
                                          (w2_raw[:].rearrange("p e c d -> p (e c d)"), w2_hi, w2_in)):
                    sc.wait_ge(arrived, 16 * E // 2)
                    for q in range(4):
                        part = slice(q * E * H // 4, (q + 1) * E * H // 4)
                        nc.scalar.copy(dst[:, part], src[:, part]).then_inc(w_hi_done, 1)

            def expert_step(stages, c, b, i):
                if 1 in stages:
                    G, k = nth(c - 1, i), (c - 1) % 2
                    sc.wait_ge(h_ready, G + 1)
                    if c - 1 >= 2:
                        sc.wait_ge(aT_ready, G - 1)
                    nc.scalar.activation(act[k][:], h_ps[k][:], ACT.Gelu).then_inc(act_ready, 1)
                if 2 in stages:
                    G, k = nth(c - 2, i), (c - 2) % 2
                    sc.wait_ge(aT_ready, G + 1)
                    if c - 2 >= 2:
                        sc.wait_ge(y_ready, G - 1)
                    nc.scalar.copy(aT_hi[k][:], aT_ps[k][:]).then_inc(ahi_ready, 1)

            def attend(a):
                for h in range(2):
                    copy_nT(NORM_OF_ATTEND[a], h)
                for h in range(2):
                    B = 2 * a + h
                    sc.wait_ge(q_written, B + 1)
                    if B:
                        sc.wait_ge(scored, HALF * B)
                    nc.scalar.copy(QT[:], q_ps[:]).then_inc(q_copied, 1)
                    sc.wait_ge(nT_used, 2 * NORM_OF_ATTEND[a] + h + 1)
                    if B:
                        sc.wait_ge(o_written, HALF * B)
                    nc.scalar.copy(V[:].rearrange("p t d -> p (t d)"), v_ps[:]).then_inc(v_copied, 1)

                    def soften(i):
                        Q, w = HALF * B + i, (i + 1) * P
                        sc.wait_ge(bias_ready, Q + 1)
                        if Q >= 2:
                            sc.wait_ge(pT_written, Q - 1)
                        nc.scalar.activation(probs[Q % 2][:, 0:w], s_ps[Q % 2][:, 0:w], ACT.Exp,
                                             bias=exp_bias[:, Q:Q + 1], scale=SCORE_SCALE,
                                             accum_out=row_sum[:, Q:Q + 1]).then_inc(exped, 1)

                    def copy_pT(i):
                        Q, w = HALF * B + i, (i + 1) * P
                        sc.wait_ge(pT_written, Q + 1)
                        if Q:
                            sc.wait_ge(o_written, Q)
                        nc.scalar.copy(probs_T[:, 0:w], pT_ps[:, 0:w]).then_inc(pT_copied, 1)

                    soften(0)
                    for i in range(HALF):
                        if i + 1 < HALF:
                            soften(i + 1)
                        copy_pT(i)

            sc.wait_ge(router_T_ps, 1)
            nc.scalar.copy(router_T[:], router_ps[:, 0:E]).then_inc(router_T_sb, 1)
            route(0)
            route(1)
            split_weights()
            run_steps(sc, 0, expert_step)
            run_steps(sc, 1, expert_step)
            attend(0)
            route(2)
            attend(1)
            route(3)
            run_steps(sc, 2, expert_step)
            run_steps(sc, 3, expert_step)

        @block.vector
        def _(dve):
            v = nc.vector
            steps = [0]

            def then(ins):
                ins.then_inc(dve_step, 1)
                steps[0] += 1
                dve.wait_ge(dve_step, steps[0])
                return ins

            def normalise(n, g):
                t0 = g * GT
                for t in range(GT):
                    last = v.bn_stats(stats[:, t, :], xs[:, t0 + t, :])
                then(last)
                for t in range(GT):
                    last = v.bn_aggr(moments[:, t, :], stats[:, t, :])
                then(last)
                then(v.tensor_scalar(var_eps[:], moments[:, :, 1], LN_EPS, None, ALU.add))
                then(v.tensor_scalar(half_bits[:], var_eps[:].bitcast(I32), 1, None, ALU.logical_shift_right))
                then(v.tensor_scalar(rstd[:].bitcast(I32), half_bits[:], -1.0, RSQRT_MAGIC, ALU.mult, ALU.add))
                for _ in range(NEWTON_STEPS):
                    then(v.tensor_tensor(newton[:], rstd[:], rstd[:], ALU.mult))
                    then(v.scalar_tensor_tensor(newton[:], newton[:], -0.5, var_eps[:], ALU.mult, ALU.mult))
                    then(v.scalar_tensor_tensor(rstd[:], newton[:], 1.5, rstd[:], ALU.add, ALU.mult))
                for t in range(GT):
                    v.tensor_scalar(xn[g][:, t, :], xs[:, t0 + t, :], moments[:, t, 0:1], rstd[:, t:t + 1],
                                    ALU.subtract, ALU.mult).then_inc(normed, 1)

            def per_tile(a):
                return a[:].unsqueeze(2).to_broadcast([P, GT, E])

            def pick(scores, chosen):
                then(v.tensor_reduce(top[:], scores[:], AX, ALU.max))
                then(v.tensor_tensor(key[:], scores[:], per_tile(top), ALU.is_equal))
                then(v.tensor_tensor(key[:], key[:], rev_e[:].unsqueeze(1).to_broadcast([P, GT, E]), ALU.mult))
                then(v.tensor_reduce(best[:], key[:], AX, ALU.max))
                then(v.tensor_tensor(chosen[:], key[:], per_tile(best), ALU.is_equal))

            def route(r):
                g, n = r % GROUPS, NORM_OF_ROUTE[r]
                normalise(n, g)
                dve.wait_ge(nT_used, 2 * n + 2)
                then(v.tensor_copy(logit[:], logit_ps[:, 0:GT * E].rearrange("p (t e) -> p t e", e=E)))
                then(v.tensor_reduce(top[:], logit[:], AX, ALU.max))
                v.tensor_tensor(shifted[:], logit[:], per_tile(top), ALU.subtract).then_inc(shifted_ready, 1)
                dve.wait_ge(shifted_ready, r + 1)
                pick(logit, pick1)
                then(v.scalar_tensor_tensor(logit2[:], pick1[:], MASKED, logit[:], ALU.mult, ALU.add))
                pick(logit2, pick2)
                v.tensor_tensor(picked16[:], pick1[:], pick2[:], ALU.add).then_inc(picked_ready, 1)
                dve.wait_ge(expd_ready, r + 1)
                then(v.tensor_reduce(den[:], expd[:], AX, ALU.add))
                then(v.reciprocal(prob1[:], den[:]))
                then(v.tensor_tensor(work[:], expd[:], pick2[:], ALU.mult))
                then(v.tensor_reduce(prob2[:], work[:], AX, ALU.add))
                then(v.tensor_tensor(prob2[:], prob2[:], prob1[:], ALU.mult))
                then(v.scalar_tensor_tensor(den[:], prob1[:], TOPK_EPS, prob2[:], ALU.add, ALU.add))
                then(v.reciprocal(den[:], den[:]))
                then(v.scalar_tensor_tensor(gate[g][:, 0, :], prob1[:], 0.5, den[:], ALU.mult, ALU.mult))
                then(v.scalar_tensor_tensor(gate[g][:, 1, :], prob2[:], 0.5, den[:], ALU.mult, ALU.mult))
                dve.wait_ge(ranked, r + 1)
                then(v.tensor_tensor(over[:], count_ps[:, 0:E].unsqueeze(2).to_broadcast([P, E, GT]),
                                     block_floor[:], ALU.is_gt))
                then(v.tensor_reduce(n_blocks[:], over[:], AX, ALU.add))
                then(v.tensor_tensor_scan(last_block[:], n_blocks[:], n_blocks[:], 0.0, ALU.add, ALU.bypass))
                then(v.tensor_tensor(first_block[:], last_block[:], n_blocks[:], ALU.subtract))
                then(v.scalar_tensor_tensor(
                    slot[:], first_block[:].unsqueeze(1).to_broadcast([P, GT, E]), float(P),
                    rank_ps[:, 0:GT * E].rearrange("p (t e) -> p t e", e=E), ALU.mult, ALU.add))
                for k, chosen in enumerate((pick1, pick2)):
                    then(v.tensor_tensor(work[:], slot[:], chosen[:], ALU.mult))
                    then(v.tensor_reduce(slot_f[:, k, :], work[:], AX, ALU.add))
                then(v.tensor_copy(slot_of[g][:], slot_f[:]))
                then(v.tensor_tensor(past[:], block_no[:],
                                     last_block[0:1, 0:E - 1].unsqueeze(1).to_broadcast([1, MAX_BLOCKS, E - 1]),
                                     ALU.is_ge))
                then(v.tensor_reduce(expert_f[:], past[:], AX, ALU.add))
                v.tensor_scalar(expert_at[g][:], expert_f[:], float(H), None, ALU.mult).then_inc(routed, 1)

            def split_weights():
                part_no = 0
                for src, hi, lo in ((w1_raw[:].rearrange("p e h -> p (e h)"), w1_hi, w1_lo),
                                    (w2_raw[:].rearrange("p e c d -> p (e c d)"), w2_hi, w2_lo)):
                    for q in range(4):
                        part = slice(q * E * H // 4, (q + 1) * E * H // 4)
                        part_no += 1
                        dve.wait_ge(w_hi_done, part_no)
                        v.tensor_tensor(lo[:, part], src[:, part], hi[:, part].bitcast(F32),
                                        ALU.subtract).then_inc(w_lo_done, 1)

            def expert_step(stages, c, b, i):
                if 0 in stages:
                    G, k = nth(c, i), c % 2
                    dve.wait_ge(xT_ready, G + 1)
                    if c >= 2:
                        dve.wait_ge(h_ready, G - 1)
                    v.tensor_copy(xT_hi[k][:], xT_ps[k][:, 0:P]).then_inc(xhi_ready, 1)
                    dve.wait_ge(xhi_ready, G + 1)
                    v.tensor_tensor(xT_lo[k][:], xT_ps[k][:, 0:P], xT_hi[k][:].bitcast(F32),
                                    ALU.subtract).then_inc(xlo_ready, 1)
                if 2 in stages:
                    G, k = nth(c - 2, i), (c - 2) % 2
                    dve.wait_ge(ahi_ready, G + 1)
                    if c - 2 >= 2:
                        dve.wait_ge(y_ready, G - 1)
                    v.tensor_tensor(aT_lo[k][:], aT_ps[k][:], aT_hi[k][:].bitcast(F32),
                                    ALU.subtract).then_inc(alo_ready, 1)
                if 3 in stages:
                    c3 = c - 3
                    G, k = nth(c3, i), c3 % UNROLL
                    dve.wait_ge(y_ready, G + 1)
                    if c3 >= UNROLL:
                        dve.wait_ge(y_stored[k], 16 * (uses(c3, i) - 1))
                    v.tensor_copy(yb[k][:], y_ps[c3 % 2][:, 0:D]).then_inc(y_copied, 1)

            def combine(p):
                g = p % GROUPS
                for t in range(GT):
                    tile = xs[:, g * GT + t, :]
                    dve.wait_ge(gathered[g][t], 16 * TOP * (p // GROUPS + 1))
                    then(v.scalar_tensor_tensor(tile, y_rows[g][:, t, 0, :], gate[g][:, 0, t:t + 1], tile,
                                                ALU.mult, ALU.add))
                    v.scalar_tensor_tensor(tile, y_rows[g][:, t, 1, :], gate[g][:, 1, t:t + 1], tile,
                                           ALU.mult, ALU.add).then_inc(combined, 1)
                dve.wait_ge(combined, (p + 1) * GT)

            def attend(a):
                normalise(NORM_OF_ATTEND[a], a)
                for h in range(2):
                    B = 2 * a + h
                    dve.wait_ge(k_written, B + 1)
                    if B:
                        dve.wait_ge(scored, HALF * B)
                    v.tensor_copy(KT[:], k_ps[:]).then_inc(k_copied, 1)

                    def maxima(i):
                        Q, w = HALF * B + i, (i + 1) * P
                        dve.wait_ge(scored, Q + 1)
                        then(v.reduce_max(neg_max[:, Q:Q + 1], s_ps[Q % 2][:, 0:w], AX, negate=True))
                        v.tensor_scalar(exp_bias[:, Q:Q + 1], neg_max[:, Q:Q + 1], SCORE_SCALE, None,
                                        ALU.mult).then_inc(bias_ready, 1)

                    def finish(i):
                        Q = HALF * B + i
                        dve.wait_ge(exped, Q + 1)
                        then(v.reciprocal(row_inv[:, Q:Q + 1], row_sum[:, Q:Q + 1]))
                        dve.wait_ge(o_written, Q + 1)
                        v.scalar_tensor_tensor(xs[:, Q, :], o_ps[Q % 2][:, 0:D], row_inv[:, Q:Q + 1],
                                               xs[:, Q, :], ALU.mult, ALU.add).then_inc(attended, 1)

                    maxima(0)
                    for i in range(HALF):
                        if i + 1 < HALF:
                            maxima(i + 1)
                        finish(i)
                dve.wait_ge(attended, GT * (a + 1))

            dve.wait_ge(consts, 12)
            dve.wait_ge(x_in[0], 32)
            route(0)
            dve.wait_ge(x_in[1], 32)
            route(1)
            split_weights()
            run_steps(dve, 0, expert_step)
            run_steps(dve, 1, expert_step)
            dve.wait_ge(scattered[0], 16 * TOP * GT)
            combine(0)
            attend(0)
            route(2)
            dve.wait_ge(scattered[1], 16 * TOP * GT)
            combine(1)
            attend(1)
            route(3)
            run_steps(dve, 2, expert_step)
            run_steps(dve, 3, expert_step)
            combine(2)
            combine(3)

        @block.tensor
        def _(pe):
            def transpose_normed(n, g):
                for h in range(2):
                    idx = 2 * n + h
                    if idx >= 2:
                        pe.wait_ge(nT_copied, idx - 1)
                    for t in range(HALF):
                        pe.wait_ge(normed, n * GT + h * HALF + t + 1)
                        mm = nc.tensor.transpose(nT_ps[h][:, t * P:(t + 1) * P], xn[g][:, h * HALF + t, :], ident[:])
                    mm.then_inc(nT_written, 1)

            def route(r):
                g, n = r % GROUPS, NORM_OF_ROUTE[r]
                transpose_normed(n, g)
                if r:
                    pe.wait_ge(routed, r)
                for h in range(2):
                    pe.wait_ge(nT_copied, 2 * n + h + 1)
                    for t in range(HALF):
                        c = (h * HALF + t) * E
                        mm = nc.tensor.matmul(logit_ps[:, c:c + E], nT[:, h, t * P:(t + 1) * P], router_T[:],
                                              start=True, stop=True)
                    mm.then_inc(nT_used, 1)
                pe.wait_ge(picked_ready, r + 1)
                flat = picked16[:].rearrange("p t e -> p (t e)")
                nc.tensor.matmul(rank_ps[:, 0:GT * E], before16[:], flat, start=True, stop=True,
                                 skip_group_check=True)
                for k in range(1, GT):
                    nc.tensor.matmul(rank_ps[:, k * E:GT * E], ones16[:], flat[:, 0:(GT - k) * E],
                                     start=False, stop=True, skip_group_check=True)
                for t in range(GT):
                    mm = nc.tensor.matmul(count_ps[:, 0:E], ones16[:], picked16[:, t, :], start=(t == 0), stop=(t == GT - 1))
                mm.then_inc(ranked, 1)

            def expert_phase(p):
                g = p % GROUPS

                def expert_of(b, i):
                    return pe.value_load(expert_at[g][0:1, bass.ds(b + UNROLL * i, 1)],
                                         min_val=0, max_val=(E - 1) * H)

                def step(stages, c, s, i):
                    if 0 in stages:
                        G, k = nth(c, i), c % 2
                        pe.wait_ge(x_loaded[c % UNROLL], 16 * uses(c, i))
                        if c >= 2:
                            pe.wait_ge(xlo_ready, G - 1)
                        nc.tensor.transpose(xT_ps[k][:, 0:P], xb[c % UNROLL][:], ident[:]).then_inc(xT_ready, 1)
                    if 1 in stages:
                        c1 = c - 1
                        G, k = nth(c1, i), c1 % 2
                        at = expert_of(s - 1, i)
                        pe.wait_ge(xlo_ready, G + 1)
                        if c1 >= 2:
                            pe.wait_ge(act_ready, G - 1)
                        hi, lo = w1_hi[:, bass.ds(at, H)], w1_lo[:, bass.ds(at, H)]
                        nc.tensor.matmul(h_ps[k][:], xT_hi[k][:], hi, start=True, stop=False)
                        nc.tensor.matmul(h_ps[k][:], xT_hi[k][:], lo, start=False, stop=False)
                        nc.tensor.matmul(h_ps[k][:], xT_lo[k][:], hi, start=False, stop=True).then_inc(h_ready, 1)
                    if 2 in stages:
                        c2 = c - 2
                        G, k = nth(c2, i), c2 % 2
                        pe.wait_ge(act_ready, G + 1)
                        if c2 >= 2:
                            pe.wait_ge(alo_ready, G - 1)
                        for q in range(HC):
                            mm = nc.tensor.transpose(aT_ps[k][:, q * P:(q + 1) * P], act[k][:, q * P:(q + 1) * P], ident[:])
                        mm.then_inc(aT_ready, 1)
                    if 3 in stages:
                        c3 = c - 3
                        G, k = nth(c3, i), c3 % 2
                        at = expert_of(s - 3, i)
                        pe.wait_ge(alo_ready, G + 1)
                        if c3 >= 2:
                            pe.wait_ge(y_copied, G - 1)
                        for q in range(HC):
                            part = slice(q * P, (q + 1) * P)
                            hi, lo = w2_hi[:, bass.ds(at + q * P, D)], w2_lo[:, bass.ds(at + q * P, D)]
                            nc.tensor.matmul(y_ps[k][:, 0:D], aT_hi[k][:, part], hi, start=(q == 0), stop=False)
                            nc.tensor.matmul(y_ps[k][:, 0:D], aT_hi[k][:, part], lo, start=False, stop=False)
                            mm = nc.tensor.matmul(y_ps[k][:, 0:D], aT_lo[k][:, part], hi, start=False, stop=(q == HC - 1))
                        mm.then_inc(y_ready, 1)

                run_steps(pe, p, step)

            def attend(a):
                n = NORM_OF_ATTEND[a]
                transpose_normed(n, a)
                pe.wait_ge(nT_copied, 2 * n + 2)
                for h in range(2):
                    B = 2 * a + h
                    if B:
                        pe.wait_ge(v_copied, B)
                        pe.wait_ge(k_copied, B)
                    nc.tensor.matmul(q_ps[:], qw[:], nT[:, h, :], start=True, stop=True).then_inc(q_written, 1)
                    nc.tensor.matmul(k_ps[:], kw[:], nT[:, h, :], start=True, stop=True).then_inc(k_written, 1)
                    for t in range(HALF):
                        mm = nc.tensor.matmul(v_ps[:, t * D:(t + 1) * D], nT[:, h, t * P:(t + 1) * P], vw[:],
                                              start=True, stop=True)
                    mm.then_inc(nT_used, 1)

                    def score(i):
                        Q, w = HALF * B + i, (i + 1) * P
                        if Q >= 2:
                            pe.wait_ge(exped, Q - 1)
                        nc.tensor.matmul(s_ps[Q % 2][:, 0:w], QT[:, i * P:(i + 1) * P], KT[:, 0:w], start=True, stop=True,
                                         skip_group_check=True)
                        nc.tensor.matmul(s_ps[Q % 2][:, i * P:w], ident16[:], causal16[:], start=False, stop=True,
                                         skip_group_check=True).then_inc(scored, 1)

                    def mix(i):
                        Q = HALF * B + i
                        pe.wait_ge(exped, Q + 1)
                        if Q:
                            pe.wait_ge(pT_copied, Q)
                        for j in range(i + 1):
                            mm = nc.tensor.transpose(pT_ps[:, j * P:(j + 1) * P], probs[Q % 2][:, j * P:(j + 1) * P], ident[:])
                        mm.then_inc(pT_written, 1)
                        pe.wait_ge(pT_copied, Q + 1)
                        pe.wait_ge(v_copied, B + 1)
                        if Q >= 2:
                            pe.wait_ge(attended, Q - 1)
                        for j in range(i + 1):
                            mm = nc.tensor.matmul(o_ps[Q % 2][:, 0:D], probs_T[:, j * P:(j + 1) * P], V[:, j, :],
                                                  start=(j == 0), stop=(j == i))
                        mm.then_inc(o_written, 1)

                    pe.wait_ge(q_copied, B + 1)
                    pe.wait_ge(k_copied, B + 1)
                    score(0)
                    for i in range(HALF):
                        if i + 1 < HALF:
                            score(i + 1)
                        mix(i)

            pe.wait_ge(consts, 12)
            pe.wait_ge(router_in, 16)
            nc.tensor.transpose(router_ps[:, 0:E], router_rows[:], ident[0:E, 0:E]).then_inc(router_T_ps, 1)
            pe.wait_ge(router_T_sb, 1)
            route(0)
            route(1)
            pe.wait_ge(routed, 2)
            pe.wait_ge(w_lo_done, 8)
            expert_phase(0)
            expert_phase(1)
            pe.wait_ge(y_copied, 2 * MAX_BLOCKS)
            pe.wait_ge(attn_w_in, 48)
            attend(0)
            pe.wait_ge(attended, GT)
            route(2)
            pe.wait_ge(routed, 3)
            attend(1)
            pe.wait_ge(attended, 2 * GT)
            route(3)
            pe.wait_ge(routed, 4)
            expert_phase(2)
            expert_phase(3)


_INS = ['L0_attn_x', 'L0_attn_Qw', 'L0_attn_Kw', 'L0_attn_Vw', 'L0_ffn_router_w', 'L0_ffn_w1', 'L0_ffn_w2']


def kernel(**inputs):
    import numpy as _np
    import concourse.bacc as _bacc
    from concourse import mybir as _mybir
    from concourse.bass_utils import run_bass_kernel_spmd as _run

    nc = _bacc.Bacc("TRN2", target_bir_lowering=False, num_devices=1)
    arrays, args = {}, []
    for name in _INS:
        a = _np.ascontiguousarray(inputs[name])
        arrays[f"in_{name}"] = a
        args.append(nc.dram_tensor(f"in_{name}", a.shape, _mybir.dt.from_np(a.dtype), kind="ExternalInput").ap())
    out = nc.dram_tensor("out", inputs['L0_attn_x'].shape, _mybir.dt.float32, kind="ExternalOutput").ap()
    macaron(nc, *args, out)
    r = _run(nc, [arrays], core_ids=[0])
    return r.results[0]["out"]
```

```python
from contextlib import ExitStack
from itertools import chain

import concourse.bass as bass
from concourse import mybir

F32 = mybir.dt.float32
F32R = mybir.dt.float32r
BF16 = mybir.dt.bfloat16
I32 = mybir.dt.int32
ALU = mybir.AluOpType
ACT = mybir.ActivationFunctionType
AX = mybir.AxisListType.X

P = 128
D = 128
H = 512
E = 8
TOP = 2
BATCH, SEQ = 4, 512
TILES = BATCH * SEQ // P
GROUPS = 2
GT = TILES // GROUPS
HALF = GT // 2
HC = H // P
MAX_BLOCKS = (GT * P * TOP + (P - 1) * E) // P
LAG = 3
UNROLL = 4
HEAD = LAG + UNROLL
LOOPS = (MAX_BLOCKS - HEAD) // UNROLL
assert LOOPS * UNROLL + HEAD == MAX_BLOCKS
LONG_HEAD = HEAD + 2 * UNROLL
LN_EPS = 1e-5
TOPK_EPS = 1e-9
SCORE_SCALE = float(D) ** -0.5
MASKED = -3.0e38
RSQRT_MAGIC = float(0x5F3759DF)
NEWTON_STEPS = 3


def macaron(nc, x, q_w, k_w, v_w, router_w, w1, w2, out):
    with ExitStack() as ctx:
        def sb(name, shape, dt=F32):
            return ctx.enter_context(nc.sbuf_tensor(name, shape, dt))

        def sem(name):
            return ctx.enter_context(nc.semaphore(name))

        slots_in = [nc.dram_tensor(f"slots_in{g}", (MAX_BLOCKS * P, D), F32).ap() for g in range(GROUPS)]
        slots_out = [nc.dram_tensor(f"slots_out{g}", (MAX_BLOCKS * P, D), F32).ap() for g in range(GROUPS)]

        w1_sb, w2_sb = sb("w1_sb", [P, E * H]), sb("w2_sb", [P, E * H])
        w1_hi, w1_lo = sb("w1_hi", [P, E * H], F32R), sb("w1_lo", [P, E * H], F32R)
        qw, kw, vw = sb("qw", [P, D]), sb("kw", [P, D]), sb("vw", [P, D])
        router_rows, router_T = sb("router_rows", [E, D]), sb("router_T", [P, E])
        ident, ident16 = sb("ident", [P, P]), sb("ident16", [P, P], BF16)
        before16 = sb("before16", [P, P], BF16)
        ones16 = sb("ones16", [P, P], BF16)
        causal16 = sb("causal16", [P, P], BF16)
        rev_e = sb("rev_e", [P, E])
        block_floor = sb("block_floor", [P, E, GT])
        block_no = sb("block_no", [1, MAX_BLOCKS, E - 1])
        zeros = sb("zeros", [P, MAX_BLOCKS * D])

        xs = sb("xs", [P, TILES, D])
        xn = [sb(f"xn{g}", [P, GT, D]) for g in range(GROUPS)]
        stats = [sb(f"stats{g}", [P, GT, 6]) for g in range(GROUPS)]
        moments = sb("moments", [P, GT, 2])
        var_eps, rstd, newton = sb("var_eps", [P, GT]), sb("rstd", [P, GT]), sb("newton", [P, GT])
        half_bits = sb("half_bits", [P, GT], I32)
        nT = [sb(f"nT{g}", [P, 2, HALF * P]) for g in range(GROUPS)]

        logit, shifted, expd = sb("logit", [P, GT, E]), sb("shifted", [P, GT, E]), sb("expd", [P, GT, E])
        key, logit2, work = sb("key", [P, GT, E]), sb("logit2", [P, GT, E]), sb("work", [P, GT, E])
        pick1, pick2 = sb("pick1", [P, GT, E]), sb("pick2", [P, GT, E])
        picked16 = sb("picked16", [P, GT, E], BF16)
        top, best = sb("top", [P, GT]), sb("best", [P, GT])
        prob1, prob2, den = sb("prob1", [P, GT]), sb("prob2", [P, GT]), sb("den", [P, GT])
        gate = [sb(f"gate{g}", [P, TOP, GT]) for g in range(GROUPS)]
        over = sb("over", [P, E, GT])
        n_blocks, last_block, first_block = sb("n_blocks", [P, E]), sb("last_block", [P, E]), sb("first_block", [P, E])
        slot = sb("slot", [P, GT, E])
        slot_f = sb("slot_f", [P, TOP, GT])
        slot_of = [sb(f"slot_of{g}", [P, TOP, GT], I32) for g in range(GROUPS)]
        past = sb("past", [1, MAX_BLOCKS, E - 1])
        expert_f = sb("expert_f", [1, MAX_BLOCKS])
        expert_at = [sb(f"expert_at{g}", [1, MAX_BLOCKS], I32) for g in range(GROUPS)]

        xb = [sb(f"xb{k}", [P, D]) for k in range(UNROLL)]
        xT_hi = [sb(f"xT_hi{k}", [P, P], F32R) for k in range(2)]
        xT_lo = [sb(f"xT_lo{k}", [P, P], F32R) for k in range(2)]
        act = [sb(f"act{k}", [P, H]) for k in range(2)]
        aT = [sb(f"aT{k}", [P, H]) for k in range(2)]
        yb = [sb(f"yb{k}", [P, D]) for k in range(UNROLL)]
        y_rows = [sb(f"y_rows{g}", [P, GT, TOP, D]) for g in range(GROUPS)]

        QT, KT = [sb(f"QT{h}", [P, SEQ]) for h in range(2)], [sb(f"KT{h}", [P, SEQ]) for h in range(2)]
        V = [sb(f"V{h}", [P, HALF, D]) for h in range(2)]
        probs = [[sb(f"probs{h}{k}", [P, SEQ]) for k in range(2)] for h in range(2)]
        probs_T = [sb(f"probs_T{h}", [P, SEQ]) for h in range(2)]
        neg_max, exp_bias = sb("neg_max", [P, TILES]), sb("exp_bias", [P, TILES])
        row_sum, row_inv = sb("row_sum", [P, TILES]), sb("row_inv", [P, TILES])

        bank = [ctx.enter_context(nc.psum_tensor(f"bank{k}", [P, 512], F32)) for k in range(8)]
        xT_ps, y_ps, h_ps, aT_ps = bank[0], bank[1], bank[2:4], bank[4:6]
        router_ps, route_ps = bank[6], bank[7]
        logit_ps, rank_ps = route_ps[:, 0:GT * E], route_ps[:, GT * E:2 * GT * E]
        count_ps = route_ps[:, 2 * GT * E:2 * GT * E + E]
        q_ps, k_ps, v_ps = [bank[2], bank[5]], [bank[3], bank[6]], bank[4]
        s_ps, pT_ps, o_ps = [bank[2:4], bank[5:7]], [bank[4], bank[7]], bank[0:2]

        x_in = [[sem(f"x_in{g}{h}") for h in range(2)] for g in range(GROUPS)]
        router_in, attn_w_in, w1_in, w2_in = sem("router_in"), sem("attn_w_in"), sem("w1_in"), sem("w2_in")
        consts, zeros_set, slots_zeroed = sem("consts"), sem("zeros_set"), sem("slots_zeroed")
        router_T_ps, router_T_sb = sem("router_T_ps"), sem("router_T_sb")
        w_hi_done, w_lo_done = sem("w_hi_done"), sem("w_lo_done")
        dve_step = sem("dve_step")
        normed, nT_written, nT_copied = sem("normed"), sem("nT_written"), sem("nT_copied")
        logits_ready = sem("logits_ready")
        shifted_ready, expd_ready = sem("shifted_ready"), sem("expd_ready")
        picked_ready, ranked = sem("picked_ready"), sem("ranked")
        slotted, routed = sem("slotted"), sem("routed")
        scattered = [sem(f"scattered{g}") for g in range(GROUPS)]
        gathered = [[sem(f"gathered{g}_{t}") for t in range(GT)] for g in range(GROUPS)]
        x_loaded = [sem(f"x_loaded{k}") for k in range(UNROLL)]
        y_stored = [sem(f"y_stored{k}") for k in range(UNROLL)]
        xT_ready, xhi_ready, xlo_ready = sem("xT_ready"), sem("xhi_ready"), sem("xlo_ready")
        h_ready, act_ready, aT_ready = sem("h_ready"), sem("act_ready"), sem("aT_ready")
        aT_copied, y_ready, y_copied = sem("aT_copied"), sem("y_ready"), sem("y_copied")
        def pair(name):
            return [sem(f"{name}{h}") for h in range(2)]

        q_written, k_written, v_written = pair("q_written"), pair("k_written"), pair("v_written")
        q_copied, k_copied, v_copied = pair("q_copied"), pair("k_copied"), pair("v_copied")
        scored, bias_ready, exped = pair("scored"), pair("bias_ready"), pair("exped")
        pT_written, pT_copied = pair("pT_written"), pair("pT_copied")
        o_written, attended = pair("o_written"), pair("attended")
        counted = sem("counted")
        combined, out_stored = sem("combined"), sem("out_stored")

        block = ctx.enter_context(nc.Block())

        NORM_OF_ROUTE = [0, 1, 3, 5]
        NORM_OF_ATTEND = [2, 4]

        def nT_ps(n, h):
            return bank[6] if n == NORM_OF_ROUTE[3] else bank[h]

        def group_of_norm(n):
            return NORM_OF_ROUTE.index(n) % GROUPS if n in NORM_OF_ROUTE else NORM_OF_ATTEND.index(n)

        TRANSPOSES_BESIDE = 4
        LOGITS_BESIDE = 6
        RANKS_BESIDE = 10
        FIRST_RANKS_BESIDE = 3

        def nth(c, i):
            return c + UNROLL * i

        def uses(c, i):
            return c // UNROLL + 1 + i

        def run_steps(eng, p, step, load_offsets=None, head=HEAD, beside=None):
            base = p * MAX_BLOCKS

            def steps(first, n, i):
                more = []
                if load_offsets:
                    b0, b1 = max(first - LAG, 0), min(first + n - 1, MAX_BLOCKS)
                    more = [dict(zip(range(b0, b1), load_offsets(b0 + UNROLL * i, b1 - b0)))]
                for s in range(first, first + n):
                    last = s - MAX_BLOCKS if first >= MAX_BLOCKS else -1
                    step([L for L in range(LAG + 1) if last < L <= s], base + s, s, i, *more)
                    if beside and (s < head or s >= MAX_BLOCKS):
                        beside(s)

            steps(0, HEAD, 0)
            for first in range(HEAD, head, UNROLL):
                steps(first, UNROLL, 0)
            with eng.Fori(0, (MAX_BLOCKS - head) // UNROLL) as i:
                steps(head, UNROLL, i)
            steps(MAX_BLOCKS, LAG, 0)

        @block.sync
        def _(sp):
            x_tiles = x.rearrange("b (t p) d -> p (b t) d", p=P)
            for g in range(GROUPS):
                for h in range(2):
                    t0 = g * GT + h * HALF
                    sp.dma_start(xs[:, t0:t0 + HALF, :], x_tiles[:, t0:t0 + HALF, :]).then_inc(x_in[g][h], 16)
                if g == 0:
                    sp.dma_start(router_rows[:], router_w).then_inc(router_in, 16)
            for e in range(0, E, 2):
                sp.dma_start(w1_sb[:, e * H:(e + 2) * H].rearrange("d (e h) -> d e h", h=H),
                             w1[e:e + 2].rearrange("e d h -> d e h")).then_inc(w1_in, 16)
            for e in range(0, E, 2):
                sp.dma_start(w2_sb[:, e * H:(e + 2) * H].rearrange("p (e c d) -> p e c d", c=HC, d=D),
                             w2[e:e + 2].rearrange("e (c p) d -> p e c d", p=P)).then_inc(w2_in, 16)
            for dst, src in ((qw, q_w), (kw, k_w), (vw, v_w)):
                sp.dma_start(dst[:], src).then_inc(attn_w_in, 16)

            def load(g, b, c, i):
                k = c % UNROLL
                if c >= UNROLL:
                    sp.wait_ge(xT_ready, nth(c, i) - UNROLL + 1)
                sp.dma_start(xb[k][:], slots_in[g][bass.ds(b * P, P), :]).then_inc(x_loaded[k], 16)

            def store(g, b, c, i):
                k = c % UNROLL
                sp.wait_ge(y_copied, nth(c, i) + 1)
                sp.dma_start(slots_out[g][bass.ds(b * P, P), :], yb[k][:]).then_inc(y_stored[k], 16)

            def expert_phase(p):
                g = p % GROUPS
                base = p * MAX_BLOCKS
                sp.wait_ge(scattered[g], 16 * TOP * GT * (p // GROUPS + 1))
                for b in range(UNROLL):
                    load(g, b, base + b, 0)

                def step(b, i):
                    if b + UNROLL < MAX_BLOCKS:
                        load(g, b + UNROLL + UNROLL * i, base + b + UNROLL, i)
                    if b >= LAG:
                        store(g, b - LAG + UNROLL * i, base + b - LAG, i)

                for b in range(HEAD):
                    step(b, 0)
                with sp.Fori(0, LOOPS - 1) as i:
                    for j in range(UNROLL):
                        step(HEAD + j, i)
                for b in range(HEAD + UNROLL * (LOOPS - 1), MAX_BLOCKS + LAG):
                    step(b, 0)

            for p in range(2 * GROUPS):
                expert_phase(p)
            o_tiles = out.rearrange("b (t p) d -> p (b t) d", p=P)
            for g in range(GROUPS):
                for h in range(2):
                    t0 = g * GT + h * HALF
                    sp.wait_ge(combined, (GROUPS + g) * GT + (h + 1) * HALF)
                    sp.dma_start(o_tiles[:, t0:t0 + HALF, :], xs[:, t0:t0 + HALF, :]).then_inc(out_stored, 16)
            sp.wait_ge(out_stored, 16 * 2 * GROUPS)

        @block.gpsimd
        def _(pool):
            pool.memset(zeros[:], 0.0).then_inc(zeros_set, 1)
            pool.memset(ident[:], 0.0).then_inc(consts, 1)
            pool.memset(ident16[:], 0.0).then_inc(consts, 1)
            pool.memset(before16[:], 1.0).then_inc(consts, 1)
            pool.memset(ones16[:], 1.0).then_inc(consts, 1)
            pool.memset(causal16[:], 0.0).then_inc(consts, 1)
            pool.wait_ge(consts, 5)
            for m in (ident, ident16):
                pool.affine_select(out=m[:], in_=m[:], compare_op=ALU.not_equal, fill=1.0, base=0,
                                   pattern=[[-1, P]], channel_multiplier=1).then_inc(consts, 1)
            pool.affine_select(out=before16[:], in_=before16[:], compare_op=ALU.is_gt, fill=0.0, base=0,
                               pattern=[[1, P]], channel_multiplier=-1).then_inc(consts, 1)
            pool.affine_select(out=causal16[:], in_=causal16[:], compare_op=ALU.is_ge, fill=MASKED, base=0,
                               pattern=[[-1, P]], channel_multiplier=1).then_inc(consts, 1)
            pool.iota(rev_e[:], [[-1, E]], base=E, channel_multiplier=0,
                      allow_small_or_imprecise_dtypes=True).then_inc(consts, 1)
            pool.iota(block_floor[:], [[0, E], [P, GT]], base=0, channel_multiplier=0,
                      allow_small_or_imprecise_dtypes=True).then_inc(consts, 1)
            pool.iota(block_no[:], [[1, MAX_BLOCKS], [0, E - 1]], base=0, channel_multiplier=0,
                      allow_small_or_imprecise_dtypes=True).then_inc(consts, 1)
            pool.wait_ge(zeros_set, 1)
            for g in range(GROUPS):
                pool.dma_start(slots_in[g].rearrange("(p n) d -> p (n d)", p=P), zeros[:]).then_inc(slots_zeroed, 16)
            pool.wait_ge(slots_zeroed, 16 * GROUPS)

            def scatter(r):
                g = r % GROUPS
                pool.wait_ge(slotted, r + 1)
                for t in range(GT):
                    for k in range(TOP):
                        pool.indirect_dma_start(
                            slots_in[g], bass.IndirectOffsetOnAxis(ap=slot_of[g][:, k, t:t + 1], axis=0),
                            xn[g][:, t, :], None).then_inc(scattered[g], 16)

            def gather(p):
                g = p % GROUPS
                for k in range(UNROLL):
                    done = len([G for G in range((p + 1) * MAX_BLOCKS) if G % UNROLL == k])
                    pool.wait_ge(y_stored[k], 16 * done)
                for t in range(GT):
                    for k in range(TOP):
                        pool.indirect_dma_start(
                            y_rows[g][:, t, k, :], None, slots_out[g],
                            bass.IndirectOffsetOnAxis(ap=slot_of[g][:, k, t:t + 1], axis=0)
                        ).then_inc(gathered[g][t], 16)

            scatter(0)
            scatter(1)
            gather(0)
            gather(1)
            scatter(2)
            scatter(3)
            gather(2)
            gather(3)

        @block.scalar
        def _(sc):
            def copy_nT(n, h):
                g, idx = group_of_norm(n), 2 * n + h
                sc.wait_ge(nT_written, idx + 1)
                nc.scalar.copy(nT[g][:, h, :], nT_ps(n, h)[:]).then_inc(nT_copied, 1)

            def exp_logits(r):
                sc.wait_ge(shifted_ready, r + 1)
                nc.scalar.activation(expd[:], shifted[:], ACT.Exp).then_inc(expd_ready, 1)

            def split_weights():
                for q in range(E // 2):
                    part = slice(2 * q * H, 2 * (q + 1) * H)
                    sc.wait_ge(w1_in, 16 * E // 2)
                    nc.scalar.copy(w1_hi[:, part], w1_sb[:, part]).then_inc(w_hi_done, 1)

            def expert_step(stages, c, s, i):
                if 1 in stages:
                    G, k = nth(c - 1, i), (c - 1) % 2
                    sc.wait_ge(h_ready, G + 1)
                    if c - 1 >= 2:
                        sc.wait_ge(aT_ready, G - 1)
                    nc.scalar.activation(act[k][:], h_ps[k][:], ACT.Gelu).then_inc(act_ready, 1)
                if 2 in stages:
                    G, k = nth(c - 2, i), (c - 2) % 2
                    sc.wait_ge(aT_ready, G + 1)
                    if c - 2 >= 2:
                        sc.wait_ge(y_ready, G - 1)
                    nc.scalar.copy(aT[k][:], aT_ps[k][:]).then_inc(aT_copied, 1)

            def project(a):
                for h in range(2):
                    sc.wait_ge(q_written[h], a + 1)
                    nc.scalar.copy(QT[h][:], q_ps[h][:]).then_inc(q_copied[h], 1)
                    sc.wait_ge(v_written[h], a + 1)
                    nc.scalar.copy(V[h][:].rearrange("p t d -> p (t d)"), v_ps[:]).then_inc(v_copied[h], 1)

            def attend(a):
                def soften(i, h):
                    n, t, w = HALF * a + i, GT * a + HALF * h + i, (i + 1) * P
                    sc.wait_ge(bias_ready[h], n + 1)
                    if n >= 2:
                        sc.wait_ge(pT_written[h], n - 1)
                    nc.scalar.activation(probs[h][n % 2][:, 0:w], s_ps[h][n % 2][:, 0:w], ACT.Exp,
                                         bias=exp_bias[:, t:t + 1], scale=SCORE_SCALE,
                                         accum_out=row_sum[:, t:t + 1]).then_inc(exped[h], 1)

                def copy_pT(i, h):
                    n, w = HALF * a + i, (i + 1) * P
                    sc.wait_ge(pT_written[h], n + 1)
                    if n:
                        sc.wait_ge(o_written[h], n)
                    nc.scalar.copy(probs_T[h][:, 0:w], pT_ps[h][:, 0:w]).then_inc(pT_copied[h], 1)

                units = [(i, h) for i in range(HALF) for h in range(2)]
                soften(*units[0])
                soften(*units[1])
                for u in range(GT):
                    if u + 2 < GT:
                        soften(*units[u + 2])
                    copy_pT(*units[u])

            def copy_both(n):
                copy_nT(n, 0)
                copy_nT(n, 1)

            sc.wait_ge(router_T_ps, 1)
            nc.scalar.copy(router_T[:], router_ps[:, 0:E]).then_inc(router_T_sb, 1)
            copy_both(NORM_OF_ROUTE[0])
            exp_logits(0)
            split_weights()
            copy_both(NORM_OF_ROUTE[1])
            exp_logits(1)
            run_steps(sc, 0, expert_step)
            run_steps(sc, 1, expert_step)
            copy_both(NORM_OF_ATTEND[0])
            project(0)
            attend(0)
            copy_both(NORM_OF_ROUTE[2])
            exp_logits(2)
            copy_both(NORM_OF_ATTEND[1])
            project(1)
            attend(1)

            def route_last(s):
                if s == TRANSPOSES_BESIDE:
                    copy_nT(NORM_OF_ROUTE[3], 0)
                if s == TRANSPOSES_BESIDE + 1:
                    copy_nT(NORM_OF_ROUTE[3], 1)
                if s == TRANSPOSES_BESIDE + 4:
                    exp_logits(3)

            run_steps(sc, 2, expert_step, head=LONG_HEAD, beside=route_last)
            run_steps(sc, 3, expert_step)

        @block.vector
        def _(dve):
            v = nc.vector
            steps = [0]
            counts = [0]

            def then(ins):
                ins.then_inc(dve_step, 1)
                steps[0] += 1
                dve.wait_ge(dve_step, steps[0])
                return ins

            def tile_stats(t):
                v.bn_stats(stats[t // GT][:, t % GT, :], xs[:, t, :]).then_inc(counted, 1)
                counts[0] += 1


            def normalise(n):
                g = group_of_norm(n)
                t0 = g * GT
                dve.wait_ge(counted, counts[0])
                for t in range(GT):
                    last = v.bn_aggr(moments[:, t, :], stats[g][:, t, :])
                then(last)
                then(v.tensor_scalar(var_eps[:], moments[:, :, 1], LN_EPS, None, ALU.add))
                then(v.tensor_scalar(half_bits[:], var_eps[:].bitcast(I32), 1, None, ALU.logical_shift_right))
                then(v.tensor_scalar(rstd[:].bitcast(I32), half_bits[:], -1.0, RSQRT_MAGIC, ALU.mult, ALU.add))
                yield
                for k in range(NEWTON_STEPS):
                    then(v.tensor_tensor(newton[:], rstd[:], rstd[:], ALU.mult))
                    then(v.scalar_tensor_tensor(newton[:], newton[:], -0.5, var_eps[:], ALU.mult, ALU.mult))
                    then(v.scalar_tensor_tensor(rstd[:], newton[:], 1.5, rstd[:], ALU.add, ALU.mult))
                    if k == 1:
                        yield
                for t in range(GT):
                    if t == 1 or t == 5:
                        yield
                    v.tensor_scalar(xn[g][:, t, :], xs[:, t0 + t, :], moments[:, t, 0:1], rstd[:, t:t + 1],
                                    ALU.subtract, ALU.mult).then_inc(normed, 1)
                dve.wait_ge(normed, (n + 1) * GT)
                yield

            def per_tile(a):
                return a[:].unsqueeze(2).to_broadcast([P, GT, E])

            def pick(scores, chosen):
                then(v.tensor_reduce(top[:], scores[:], AX, ALU.max))
                then(v.tensor_tensor(key[:], scores[:], per_tile(top), ALU.is_equal))
                then(v.tensor_tensor(key[:], key[:], rev_e[:].unsqueeze(1).to_broadcast([P, GT, E]), ALU.mult))
                then(v.tensor_reduce(best[:], key[:], AX, ALU.max))
                then(v.tensor_tensor(chosen[:], key[:], per_tile(best), ALU.is_equal))

            def route(r):
                g = r % GROUPS
                dve.wait_ge(logits_ready, r + 1)
                then(v.tensor_copy(logit[:], logit_ps.rearrange("p (t e) -> p t e", e=E)))
                then(v.tensor_reduce(top[:], logit[:], AX, ALU.max))
                v.tensor_tensor(shifted[:], logit[:], per_tile(top), ALU.subtract).then_inc(shifted_ready, 1)
                dve.wait_ge(shifted_ready, r + 1)
                yield
                pick(logit, pick1)
                yield
                then(v.scalar_tensor_tensor(logit2[:], pick1[:], MASKED, logit[:], ALU.mult, ALU.add))
                pick(logit2, pick2)
                v.tensor_tensor(picked16[:], pick1[:], pick2[:], ALU.add).then_inc(picked_ready, 1)
                yield
                yield
                dve.wait_ge(ranked, r + 1)
                then(v.tensor_tensor(over[:], count_ps.unsqueeze(2).to_broadcast([P, E, GT]),
                                     block_floor[:], ALU.is_gt))
                then(v.tensor_reduce(n_blocks[:], over[:], AX, ALU.add))
                then(v.tensor_tensor_scan(last_block[:], n_blocks[:], n_blocks[:], 0.0, ALU.add, ALU.bypass))
                then(v.tensor_tensor(first_block[:], last_block[:], n_blocks[:], ALU.subtract))
                then(v.scalar_tensor_tensor(
                    slot[:], first_block[:].unsqueeze(1).to_broadcast([P, GT, E]), float(P),
                    rank_ps.rearrange("p (t e) -> p t e", e=E), ALU.mult, ALU.add))
                yield
                for k, chosen in enumerate((pick1, pick2)):
                    then(v.tensor_tensor(work[:], slot[:], chosen[:], ALU.mult))
                    then(v.tensor_reduce(slot_f[:, k, :], work[:], AX, ALU.add))
                v.tensor_copy(slot_of[g][:], slot_f[:]).then_inc(slotted, 1)
                yield
                then(v.tensor_tensor(past[:], block_no[:],
                                     last_block[0:1, 0:E - 1].unsqueeze(1).to_broadcast([1, MAX_BLOCKS, E - 1]),
                                     ALU.is_ge))
                then(v.tensor_reduce(expert_f[:], past[:], AX, ALU.add))
                v.tensor_scalar(expert_at[g][:], expert_f[:], float(H), None, ALU.mult).then_inc(routed, 1)
                dve.wait_ge(routed, r + 1)
                yield

            def gates(r):
                g = r % GROUPS
                dve.wait_ge(expd_ready, r + 1)
                then(v.tensor_reduce(den[:], expd[:], AX, ALU.add))
                then(v.reciprocal(prob1[:], den[:]))
                then(v.tensor_tensor(work[:], expd[:], pick2[:], ALU.mult))
                then(v.tensor_reduce(prob2[:], work[:], AX, ALU.add))
                yield
                then(v.tensor_tensor(prob2[:], prob2[:], prob1[:], ALU.mult))
                then(v.scalar_tensor_tensor(den[:], prob1[:], TOPK_EPS, prob2[:], ALU.add, ALU.add))
                then(v.reciprocal(den[:], den[:]))
                then(v.scalar_tensor_tensor(gate[g][:, 0, :], prob1[:], 0.5, den[:], ALU.mult, ALU.mult))
                then(v.scalar_tensor_tensor(gate[g][:, 1, :], prob2[:], 0.5, den[:], ALU.mult, ALU.mult))
                yield

            def beside(pieces):
                return lambda s: next(pieces, None)

            def rest(pieces):
                for _ in pieces:
                    pass

            def split_weights():
                for q in range(E // 2):
                    part = slice(2 * q * H, 2 * (q + 1) * H)
                    dve.wait_ge(w_hi_done, q + 1)
                    v.tensor_tensor(w1_lo[:, part], w1_sb[:, part], w1_hi[:, part].bitcast(F32),
                                    ALU.subtract).then_inc(w_lo_done, 1)

            def expert_step(stages, c, s, i):
                if 0 in stages:
                    G, k = nth(c, i), c % 2
                    dve.wait_ge(xT_ready, G + 1)
                    if c >= 2:
                        dve.wait_ge(h_ready, G - 1)
                    v.tensor_copy(xT_hi[k][:], xT_ps[:, 0:P]).then_inc(xhi_ready, 1)
                    dve.wait_ge(xhi_ready, G + 1)
                    v.tensor_tensor(xT_lo[k][:], xT_ps[:, 0:P], xT_hi[k][:].bitcast(F32),
                                    ALU.subtract).then_inc(xlo_ready, 1)
                if 3 in stages:
                    c3 = c - 3
                    G, k = nth(c3, i), c3 % UNROLL
                    dve.wait_ge(y_ready, G + 1)
                    if c3 >= UNROLL:
                        dve.wait_ge(y_stored[k], 16 * (uses(c3, i) - 1))
                    v.tensor_copy(yb[k][:], y_ps[:, 0:D]).then_inc(y_copied, 1)

            def combine(p, t):
                g = p % GROUPS
                tile = xs[:, g * GT + t, :]
                dve.wait_ge(gathered[g][t], 16 * TOP * (p // GROUPS + 1))
                then(v.scalar_tensor_tensor(tile, y_rows[g][:, t, 0, :], gate[g][:, 0, t:t + 1], tile,
                                            ALU.mult, ALU.add))
                v.scalar_tensor_tensor(tile, y_rows[g][:, t, 1, :], gate[g][:, 1, t:t + 1], tile,
                                       ALU.mult, ALU.add).then_inc(combined, 1)

            def combine_and_count(p, t):
                combine(p, t)
                dve.wait_ge(combined, p * GT + t + 1)
                tile_stats(p * GT + t)

            def copy_keys(a):
                for h in range(2):
                    dve.wait_ge(k_written[h], a + 1)
                    v.tensor_copy(KT[h][:], k_ps[h][:]).then_inc(k_copied[h], 1)

            def attend(a, beside):
                def maxima(i, h):
                    n, t, w = HALF * a + i, GT * a + HALF * h + i, (i + 1) * P
                    dve.wait_ge(scored[h], n + 1)
                    then(v.reduce_max(neg_max[:, t:t + 1], s_ps[h][n % 2][:, 0:w], AX, negate=True))
                    v.tensor_scalar(exp_bias[:, t:t + 1], neg_max[:, t:t + 1], SCORE_SCALE, None,
                                    ALU.mult).then_inc(bias_ready[h], 1)

                def finish(i, h):
                    n, t = HALF * a + i, GT * a + HALF * h + i
                    dve.wait_ge(exped[h], n + 1)
                    then(v.reciprocal(row_inv[:, t:t + 1], row_sum[:, t:t + 1]))
                    dve.wait_ge(o_written[h], n + 1)
                    v.scalar_tensor_tensor(xs[:, t, :], o_ps[h][:, 0:D], row_inv[:, t:t + 1],
                                           xs[:, t, :], ALU.mult, ALU.add).then_inc(attended[h], 1)
                    beside(2 * i + h)
                    dve.wait_ge(attended[h], n + 1)
                    tile_stats(t)

                units = [(i, h) for i in range(HALF) for h in range(2)]
                for u in range(3):
                    maxima(*units[u])
                for u in range(GT):
                    if u + 3 < GT:
                        maxima(*units[u + 3])
                    finish(*units[u])

            dve.wait_ge(consts, 12)
            for t in range(GT):
                if t % HALF == 0:
                    dve.wait_ge(x_in[0][t // HALF], 16)
                tile_stats(t)
            rest(normalise(NORM_OF_ROUTE[0]))
            rest(route(0))
            split_weights()
            rest(gates(0))
            for t in range(GT):
                if t % HALF == 0:
                    dve.wait_ge(x_in[1][t // HALF], 16)
                tile_stats(GT + t)
            rest(normalise(NORM_OF_ROUTE[1]))
            pieces = chain(route(1), gates(1))
            run_steps(dve, 0, expert_step, head=LONG_HEAD, beside=beside(pieces))
            rest(pieces)
            dve.wait_ge(scattered[0], 16 * TOP * GT)
            norm_pieces = chain(normalise(NORM_OF_ATTEND[0]))

            def first_group(s):
                t = s - (LONG_HEAD - GT)
                if 0 <= t < GT:
                    combine_and_count(0, t)
                if s >= MAX_BLOCKS:
                    next(norm_pieces, None)

            run_steps(dve, 1, expert_step, head=LONG_HEAD, beside=first_group)
            rest(norm_pieces)
            copy_keys(0)
            attend(0, lambda u: combine_and_count(1, u - HALF) if u >= HALF else None)
            rest(normalise(NORM_OF_ROUTE[2]))
            for t in range(HALF, GT):
                combine_and_count(1, t)
            rest(route(2))
            dve.wait_ge(scattered[1], 16 * TOP * GT)
            rest(normalise(NORM_OF_ATTEND[1]))
            copy_keys(1)
            attend(1, beside(gates(2)))
            pieces = chain(normalise(NORM_OF_ROUTE[3]), (None for _ in range(LOGITS_BESIDE - 4)),
                           route(3), gates(3))
            run_steps(dve, 2, expert_step, head=LONG_HEAD, beside=beside(pieces))
            rest(pieces)
            run_steps(dve, 3, expert_step)
            for p in (2, 3):
                for t in range(GT):
                    combine(p, t)

        @block.tensor
        def _(pe):
            offset_regs = [pe.alloc_register(f"offset{n}") for n in range(HEAD - 1)]

            def transpose_normed(n, h):
                g, idx = group_of_norm(n), 2 * n + h
                if idx >= 2:
                    pe.wait_ge(nT_copied, idx - 1)
                if n == NORM_OF_ROUTE[3] and h:
                    pe.wait_ge(nT_copied, idx)
                for t in range(HALF):
                    pe.wait_ge(normed, n * GT + h * HALF + t + 1)
                    mm = nc.tensor.transpose(nT_ps(n, h)[:, t * P:(t + 1) * P], xn[g][:, h * HALF + t, :], ident[:])
                mm.then_inc(nT_written, 1)

            def transpose_both(n):
                transpose_normed(n, 0)
                transpose_normed(n, 1)

            def logits(r):
                g, n = r % GROUPS, NORM_OF_ROUTE[r]
                if r:
                    pe.wait_ge(routed, r)
                for h in range(2):
                    pe.wait_ge(nT_copied, 2 * n + h + 1)
                    for t in range(HALF):
                        c = (h * HALF + t) * E
                        mm = nc.tensor.matmul(logit_ps[:, c:c + E], nT[g][:, h, t * P:(t + 1) * P], router_T[:],
                                              start=True, stop=True)
                mm.then_inc(logits_ready, 1)

            def ranks(r):
                pe.wait_ge(picked_ready, r + 1)
                flat = picked16[:].rearrange("p t e -> p (t e)")
                nc.tensor.matmul(rank_ps, before16[:], flat, start=True, stop=True, skip_group_check=True)
                for k in range(1, GT):
                    nc.tensor.matmul(rank_ps[:, k * E:GT * E], ones16[:], flat[:, 0:(GT - k) * E],
                                     start=False, stop=True, skip_group_check=True)
                for t in range(GT):
                    mm = nc.tensor.matmul(count_ps, ones16[:], picked16[:, t, :], start=(t == 0), stop=(t == GT - 1))
                mm.then_inc(ranked, 1)

            def expert_phase(p, **beside):
                g = p % GROUPS

                def load_offsets(first, n):
                    regs = offset_regs[:n]
                    pe.load(regs, expert_at[g][0:1, bass.ds(first, n)])
                    return [pe.snap(reg, min_val=0, max_val=(E - 1) * H) for reg in regs]

                def step(stages, c, s, i, offset):
                    if 0 in stages:
                        G = nth(c, i)
                        pe.wait_ge(x_loaded[c % UNROLL], 16 * uses(c, i))
                        if c >= 1:
                            pe.wait_ge(xlo_ready, G)
                        nc.tensor.transpose(xT_ps[:, 0:P], xb[c % UNROLL][:], ident[:]).then_inc(xT_ready, 1)
                    if 1 in stages:
                        c1 = c - 1
                        G, k = nth(c1, i), c1 % 2
                        at = offset[s - 1]
                        pe.wait_ge(xlo_ready, G + 1)
                        if c1 >= 2:
                            pe.wait_ge(act_ready, G - 1)
                        hi, lo = w1_hi[:, bass.ds(at, H)], w1_lo[:, bass.ds(at, H)]
                        nc.tensor.matmul(h_ps[k][:], xT_hi[k][:], hi, start=True, stop=False)
                        nc.tensor.matmul(h_ps[k][:], xT_hi[k][:], lo, start=False, stop=False)
                        nc.tensor.matmul(h_ps[k][:], xT_lo[k][:], hi, start=False, stop=True).then_inc(h_ready, 1)
                    if 2 in stages:
                        c2 = c - 2
                        G, k = nth(c2, i), c2 % 2
                        pe.wait_ge(act_ready, G + 1)
                        if c2 >= 2:
                            pe.wait_ge(aT_copied, G - 1)
                        for q in range(HC):
                            mm = nc.tensor.transpose(aT_ps[k][:, q * P:(q + 1) * P], act[k][:, q * P:(q + 1) * P], ident[:])
                        mm.then_inc(aT_ready, 1)
                    if 3 in stages:
                        c3 = c - 3
                        G, k = nth(c3, i), c3 % 2
                        at = offset[s - 3]
                        pe.wait_ge(aT_copied, G + 1)
                        if c3 >= 1:
                            pe.wait_ge(y_copied, G)
                        for q in range(HC):
                            mm = nc.tensor.matmul(y_ps[:, 0:D], aT[k][:, q * P:(q + 1) * P],
                                                  w2_sb[:, bass.ds(at + q * D, D)], start=(q == 0), stop=(q == HC - 1))
                        mm.then_inc(y_ready, 1)

                run_steps(pe, p, step, load_offsets, **beside)

            def project(a, h):
                pe.wait_ge(nT_copied, 2 * NORM_OF_ATTEND[a] + h + 1)
                x_T = nT[a][:, h, :]
                nc.tensor.matmul(q_ps[h][:], qw[:], x_T, start=True, stop=True).then_inc(q_written[h], 1)
                nc.tensor.matmul(k_ps[h][:], kw[:], x_T, start=True, stop=True).then_inc(k_written[h], 1)
                if h:
                    pe.wait_ge(v_copied[0], a + 1)
                for t in range(HALF):
                    mm = nc.tensor.matmul(v_ps[:, t * D:(t + 1) * D], x_T[:, t * P:(t + 1) * P], vw[:],
                                          start=True, stop=True)
                mm.then_inc(v_written[h], 1)

            def attend(a):
                def score(i, h):
                    n, w = HALF * a + i, (i + 1) * P
                    if i >= 2:
                        pe.wait_ge(exped[h], n - 1)
                    bank_s = s_ps[h][n % 2]
                    nc.tensor.matmul(bank_s[:, 0:w], QT[h][:, i * P:w], KT[h][:, 0:w], start=True, stop=True,
                                     skip_group_check=True)
                    nc.tensor.matmul(bank_s[:, i * P:w], ident16[:], causal16[:], start=False, stop=True,
                                     skip_group_check=True).then_inc(scored[h], 1)

                def transpose_probs(i, h):
                    n = HALF * a + i
                    pe.wait_ge(exped[h], n + 1)
                    if i:
                        pe.wait_ge(pT_copied[h], n)
                    for j in range(i + 1):
                        mm = nc.tensor.transpose(pT_ps[h][:, j * P:(j + 1) * P],
                                                 probs[h][n % 2][:, j * P:(j + 1) * P], ident[:])
                    mm.then_inc(pT_written[h], 1)

                def mix(i, h):
                    n = HALF * a + i
                    pe.wait_ge(pT_copied[h], n + 1)
                    if i:
                        pe.wait_ge(attended[h], n)
                    for j in range(i + 1):
                        mm = nc.tensor.matmul(o_ps[h][:, 0:D], probs_T[h][:, j * P:(j + 1) * P], V[h][:, j, :],
                                              start=(j == 0), stop=(j == i))
                    mm.then_inc(o_written[h], 1)

                for h in range(2):
                    pe.wait_ge(q_copied[h], a + 1)
                    pe.wait_ge(k_copied[h], a + 1)
                pe.wait_ge(v_copied[1], a + 1)
                units = [(i, h) for i in range(HALF) for h in range(2)]
                for u in range(3):
                    score(*units[u])
                transpose_probs(*units[0])
                for u in range(GT):
                    if u + 3 < GT:
                        score(*units[u + 3])
                    if u + 1 < GT:
                        transpose_probs(*units[u + 1])
                    mix(*units[u])

            pe.wait_ge(consts, 12)
            pe.wait_ge(router_in, 16)
            nc.tensor.transpose(router_ps[:, 0:E], router_rows[:], ident[0:E, 0:E]).then_inc(router_T_ps, 1)
            pe.wait_ge(router_T_sb, 1)
            transpose_both(NORM_OF_ROUTE[0])
            logits(0)
            ranks(0)
            transpose_both(NORM_OF_ROUTE[1])
            logits(1)
            pe.wait_ge(w_lo_done, E // 2)
            pe.wait_ge(w2_in, 16 * E // 2)
            expert_phase(0, head=HEAD, beside=lambda s: ranks(1) if s == FIRST_RANKS_BESIDE else None)
            pe.wait_ge(routed, 2)
            expert_phase(1)
            pe.wait_ge(y_copied, 2 * MAX_BLOCKS)
            pe.wait_ge(attn_w_in, 48)
            transpose_both(NORM_OF_ATTEND[0])
            project(0, 0)
            project(0, 1)
            attend(0)
            for h in range(2):
                pe.wait_ge(attended[h], HALF)
            transpose_both(NORM_OF_ROUTE[2])
            logits(2)
            ranks(2)
            transpose_both(NORM_OF_ATTEND[1])
            project(1, 0)
            project(1, 1)
            pe.wait_ge(routed, 3)
            attend(1)
            for h in range(2):
                pe.wait_ge(attended[h], 2 * HALF)

            def route_last(s):
                if s == TRANSPOSES_BESIDE:
                    transpose_normed(NORM_OF_ROUTE[3], 0)
                if s == TRANSPOSES_BESIDE + 1:
                    transpose_normed(NORM_OF_ROUTE[3], 1)
                if s == LOGITS_BESIDE:
                    logits(3)
                if s == RANKS_BESIDE:
                    ranks(3)

            expert_phase(2, head=LONG_HEAD, beside=route_last)
            pe.wait_ge(routed, 4)
            expert_phase(3)


_INS = ['L0_attn_x', 'L0_attn_Qw', 'L0_attn_Kw', 'L0_attn_Vw', 'L0_ffn_router_w', 'L0_ffn_w1', 'L0_ffn_w2']


def kernel(**inputs):
    import numpy as _np
    import concourse.bacc as _bacc
    from concourse import mybir as _mybir
    from concourse.bass_utils import run_bass_kernel_spmd as _run

    nc = _bacc.Bacc("TRN2", target_bir_lowering=False, num_devices=1)
    arrays, args = {}, []
    for name in _INS:
        a = _np.ascontiguousarray(inputs[name])
        arrays[f"in_{name}"] = a
        args.append(nc.dram_tensor(f"in_{name}", a.shape, _mybir.dt.from_np(a.dtype), kind="ExternalInput").ap())
    out = nc.dram_tensor("out", inputs['L0_attn_x'].shape, _mybir.dt.float32, kind="ExternalOutput").ap()
    macaron(nc, *args, out)
    r = _run(nc, [arrays], core_ids=[0])
    return r.results[0]["out"]
```

```python
from contextlib import ExitStack
from itertools import chain

import concourse.bass as bass
from concourse import mybir

F32 = mybir.dt.float32
BF16 = mybir.dt.bfloat16
I32 = mybir.dt.int32
ALU = mybir.AluOpType
ACT = mybir.ActivationFunctionType
AX = mybir.AxisListType.X

P = 128
D = 128
H = 512
E = 8
TOP = 2
BATCH, SEQ = 4, 512
TILES = BATCH * SEQ // P
GROUPS = 2
GT = TILES // GROUPS
HALF = GT // 2
HC = H // P
MAX_BLOCKS = (GT * P * TOP + (P - 1) * E) // P
LAG = 3
UNROLL = 4
HEAD = LAG + UNROLL + (MAX_BLOCKS - LAG - UNROLL) % UNROLL
MIDDLE = LAG + (MAX_BLOCKS - LAG) % UNROLL
LONG_HEAD = HEAD + 2 * UNROLL
BLOCKS = GROUPS * MAX_BLOCKS
LN_EPS = 1e-5
TOPK_EPS = 1e-9
SCORE_SCALE = float(D) ** -0.5
MASKED = -3.0e38
RSQRT_MAGIC = float(0x5F3759DF)
NEWTON_STEPS = 3


def macaron(nc, x, q_w, k_w, v_w, router_w, w1, w2, out):
    with ExitStack() as ctx:
        def sb(name, shape, dt=F32):
            return ctx.enter_context(nc.sbuf_tensor(name, shape, dt))

        def sem(name):
            return ctx.enter_context(nc.semaphore(name))

        slots_in = [nc.dram_tensor(f"slots_in{g}", (MAX_BLOCKS * P, D), F32).ap() for g in range(GROUPS)]
        slots_out = [nc.dram_tensor(f"slots_out{g}", (MAX_BLOCKS * P, D), F32).ap() for g in range(GROUPS)]

        ROWS = TOP * GT * P
        final_rows = nc.dram_tensor("final_rows", (ROWS + MAX_BLOCKS * P, D), F32).ap()
        numbered_slots = nc.dram_tensor("numbered_slots", (MAX_BLOCKS * P, D + 1), F32).ap()

        w1_sb, w2_sb = sb("w1_sb", [P, E * H]), sb("w2_sb", [P, E * H])
        qw, kw, vw = sb("qw", [P, D]), sb("kw", [P, D]), sb("vw", [P, D])
        router_rows, router_T = sb("router_rows", [E, D]), sb("router_T", [P, E])
        ident, ident16 = sb("ident", [P, P]), sb("ident16", [P, P], BF16)
        before16 = sb("before16", [P, P], BF16)
        ones16 = sb("ones16", [P, P], BF16)
        causal16 = sb("causal16", [P, P], BF16)
        rev_e = sb("rev_e", [P, E])
        block_floor = sb("block_floor", [P, E, GT])
        block_no = sb("block_no", [1, MAX_BLOCKS, E - 1])
        zeros = sb("zeros", [P, MAX_BLOCKS * D])
        numbered = sb("numbered", [P, MAX_BLOCKS, D + 1])

        xs = sb("xs", [P, TILES, D])
        xn_numbered = [sb(f"xn_numbered{k}", [P, GT, D + 1]) for k in range(TOP)]
        xn = [sb("xn0", [P, GT, D]), xn_numbered[0][:, :, 0:D]]
        stats = [sb(f"stats{g}", [P, GT, 6]) for g in range(GROUPS)]
        moments = sb("moments", [P, TILES, 2])
        var_eps, rstd, newton = sb("var_eps", [P, TILES]), sb("rstd", [P, TILES]), sb("newton", [P, TILES])
        half_bits = sb("half_bits", [P, TILES], I32)
        nT = [sb(f"nT{g}", [P, 2, HALF * P]) for g in range(GROUPS)]

        logit, shifted, expd = sb("logit", [P, GT, E]), sb("shifted", [P, GT, E]), sb("expd", [P, GT, E])
        key, logit2, work = sb("key", [P, GT, E]), sb("logit2", [P, GT, E]), sb("work", [P, GT, E])
        pick1, pick2 = sb("pick1", [P, GT, E]), sb("pick2", [P, GT, E])
        picked16 = sb("picked16", [P, GT, E], BF16)
        top, best = sb("top", [P, GT]), sb("best", [P, GT])
        prob1, prob2, den = sb("prob1", [P, GT]), sb("prob2", [P, GT]), sb("den", [P, GT])
        gate = [sb(f"gate{g}", [P, TOP, GT]) for g in range(GROUPS)]
        over = sb("over", [P, E, GT])
        n_blocks, last_block, first_block = sb("n_blocks", [P, E]), sb("last_block", [P, E]), sb("first_block", [P, E])
        slot = sb("slot", [P, GT, E])
        slot_f = sb("slot_f", [P, TOP, GT])
        slot_of = [sb(f"slot_of{g}", [P, TOP, GT], I32) for g in range(GROUPS)]
        past = sb("past", [1, MAX_BLOCKS, E - 1])
        expert_f = sb("expert_f", [1, MAX_BLOCKS])
        expert_at = sb("expert_at", [1, BLOCKS], I32)

        xb_numbered = [sb(f"xb_numbered{k}", [P, D + 1]) for k in range(UNROLL)]
        xb = [a[:, 0:D] for a in xb_numbered]
        row_of = sb("row_of", [P, MAX_BLOCKS], I32)
        xT = [sb(f"xT{k}", [P, P]) for k in range(UNROLL)]
        w1_block = [sb(f"w1_block{k}", [P, H]) for k in range(2)]
        act = [sb(f"act{k}", [P, H]) for k in range(2)]
        yb = [sb(f"yb{k}", [P, D]) for k in range(UNROLL)]
        y_rows = [sb(f"y_rows{g}", [P, GT, TOP, D]) for g in range(GROUPS)]

        QT, KT = [sb(f"QT{h}", [P, SEQ]) for h in range(2)], [sb(f"KT{h}", [P, SEQ]) for h in range(2)]
        V = [sb(f"V{h}", [P, HALF, D]) for h in range(2)]
        probs = [[sb(f"probs{h}{k}", [P, SEQ]) for k in range(2)] for h in range(2)]
        probs_T = [sb(f"probs_T{h}", [P, SEQ]) for h in range(2)]
        neg_max, exp_bias = sb("neg_max", [P, TILES]), sb("exp_bias", [P, TILES])
        row_sum, row_inv = sb("row_sum", [P, TILES]), sb("row_inv", [P, TILES])

        bank = [ctx.enter_context(nc.psum_tensor(f"bank{k}", [P, 512], F32)) for k in range(8)]
        xT_ps, h_ps, y_ps = bank[0:2], bank[2:4], bank[4:6]
        router_ps, route_ps = bank[6], bank[7]
        logit_ps, rank_ps = route_ps[:, 0:GT * E], route_ps[:, GT * E:2 * GT * E]
        count_ps = route_ps[:, 2 * GT * E:2 * GT * E + E]
        q_ps, k_ps, v_ps = [bank[2], bank[5]], [bank[3], bank[6]], bank[4]
        s_ps, pT_ps, o_ps = [bank[2:4], bank[5:7]], [bank[4], bank[7]], bank[0:2]

        x_in = [[sem(f"x_in{g}{h}") for h in range(2)] for g in range(GROUPS)]
        router_in, attn_w_in, w1_in, w2_in = sem("router_in"), sem("attn_w_in"), sem("w1_in"), sem("w2_in")
        consts, zeros_set = sem("consts"), sem("zeros_set")
        slots_zeroed = [sem(f"slots_zeroed{g}") for g in range(GROUPS)]
        router_T_ps, router_T_sb = sem("router_T_ps"), sem("router_T_sb")
        dve_step = sem("dve_step")
        normed, nT_written, nT_copied = sem("normed"), sem("nT_written"), sem("nT_copied")
        logits_ready = sem("logits_ready")
        shifted_ready, expd_ready = sem("shifted_ready"), sem("expd_ready")
        picked_ready, ranked = sem("picked_ready"), sem("ranked")
        slotted, routed = sem("slotted"), sem("routed")
        numbered_set, slots_numbered = sem("numbered_set"), sem("slots_numbered")
        second_copied, row_known = sem("second_copied"), sem("row_known")
        final_stored = [sem(f"final_stored{k}") for k in range(UNROLL)]
        final_loaded = [sem(f"final_loaded{q}") for q in range(GT // 2)]
        scattered = [sem(f"scattered{g}") for g in range(GROUPS)]
        gathered = [[sem(f"gathered{g}_{t}") for t in range(GT)] for g in range(GROUPS)]
        x_loaded = [sem(f"x_loaded{k}") for k in range(UNROLL)]
        y_stored = [sem(f"y_stored{k}") for k in range(UNROLL)]
        xT_ready, xT_copied = sem("xT_ready"), sem("xT_copied")
        w1_copied = sem("w1_copied")
        h_ready, act_ready = sem("h_ready"), sem("act_ready")
        y_ready, y_copied = sem("y_ready"), sem("y_copied")

        def pair(name):
            return [sem(f"{name}{h}") for h in range(2)]

        q_written, k_written, v_written = pair("q_written"), pair("k_written"), pair("v_written")
        q_copied, k_copied, v_copied = pair("q_copied"), pair("k_copied"), pair("v_copied")
        scored, bias_ready, exped = pair("scored"), pair("bias_ready"), pair("exped")
        pT_written, pT_copied = pair("pT_written"), pair("pT_copied")
        o_written, attended = pair("o_written"), pair("attended")
        counted = sem("counted")
        combined, out_stored = sem("combined"), sem("out_stored")

        block = ctx.enter_context(nc.Block())

        NORM_OF_ROUTE = [0, 1, 3, 5]
        NORM_OF_ATTEND = [2, 4]

        def nT_ps(n, h):
            return bank[6] if n == NORM_OF_ROUTE[3] else bank[h]

        def group_of_norm(n):
            return NORM_OF_ROUTE.index(n) % GROUPS if n in NORM_OF_ROUTE else NORM_OF_ATTEND.index(n)

        TRANSPOSES_BESIDE = 1
        LOGITS_BESIDE = 4
        RANKS_BESIDE = 7
        FIRST_RANKS_BESIDE = 1
        FIRST_COMBINE = MAX_BLOCKS + LAG + UNROLL
        FINAL_PACE = 5
        LAST_GROUP = 2 * BLOCKS - MAX_BLOCKS
        ALONE = 0

        def nth(c, i):
            return c + UNROLL * i

        def uses(c, i):
            return c // UNROLL + 1 + i

        def run_steps(eng, m, step, table=None, head=HEAD, middle=MIDDLE, beside=None, at_switch=None):
            base = m * BLOCKS

            def steps(first, n, i):
                more = []
                if table:
                    regs, lag = table
                    b0, b1 = max(first - lag, 0), min(first + n - lag, BLOCKS)
                    offsets = regs[:max(b1 - b0, 0)]
                    if offsets:
                        eng.load(offsets, expert_at[0:1, bass.ds(b0 + UNROLL * i, b1 - b0)])
                    more = [{b: eng.snap(reg, min_val=0, max_val=(E - 1) * H)
                             for b, reg in zip(range(b0, b1), offsets)}]
                for s in range(first, first + n):
                    last = s - BLOCKS if first >= BLOCKS else -1
                    step([L for L in range(LAG + 1) if last < L <= s], base + s, s, i, *more)
                    if beside and i is ALONE:
                        beside(s)

            def alone(first, end):
                for s in range(first, end, UNROLL):
                    steps(s, min(UNROLL, end - s), ALONE)

            def loop(first, end):
                if first < end:
                    with eng.Fori(0, (end - first) // UNROLL) as i:
                        steps(first, UNROLL, i)

            alone(0, head)
            loop(head, MAX_BLOCKS)
            if at_switch:
                at_switch()
            alone(MAX_BLOCKS, MAX_BLOCKS + middle)
            loop(MAX_BLOCKS + middle, BLOCKS)
            alone(BLOCKS, BLOCKS + LAG)

        @block.sync
        def _(sp):
            x_tiles = x.rearrange("b (t p) d -> p (b t) d", p=P)
            for g in range(GROUPS):
                for h in range(2):
                    t0 = g * GT + h * HALF
                    sp.dma_start(xs[:, t0:t0 + HALF, :], x_tiles[:, t0:t0 + HALF, :]).then_inc(x_in[g][h], 16)
                if g == 0:
                    sp.dma_start(router_rows[:], router_w).then_inc(router_in, 16)
            for e in range(0, E, 2):
                sp.dma_start(w1_sb[:, e * H:(e + 2) * H].rearrange("d (e h) -> d e h", h=H),
                             w1[e:e + 2].rearrange("e d h -> d e h")).then_inc(w1_in, 16)
            for e in range(0, E, 2):
                sp.dma_start(w2_sb[:, e * H:(e + 2) * H].rearrange("p (e c d) -> p e c d", c=HC, d=D),
                             w2[e:e + 2].rearrange("e (c p) d -> p e c d", p=P)).then_inc(w2_in, 16)
            for dst, src in ((qw, q_w), (kw, k_w), (vw, v_w)):
                sp.dma_start(dst[:], src).then_inc(attn_w_in, 16)

            def load(g, b, c, i):
                k = c % UNROLL
                last = c >= LAST_GROUP
                if c >= LAST_GROUP + UNROLL:
                    sp.wait_ge(row_known, c - LAST_GROUP + UNROLL * i - UNROLL + 1)
                elif c >= UNROLL:
                    sp.wait_ge(xT_ready, nth(c, i) - UNROLL + 1)
                here, source = (xb_numbered[k], numbered_slots) if last else (xb[k], slots_in[g])
                sp.dma_start(here[:], source[bass.ds(b * P, P), :]).then_inc(x_loaded[k], 16)

            def store(g, b, c, i):
                k = c % UNROLL
                sp.wait_ge(y_copied, nth(c, i) + 1)
                sp.dma_start(slots_out[g][bass.ds(b * P, P), :], yb[k][:]).then_inc(y_stored[k], 16)

            def expert_phase(m):
                base = m * BLOCKS

                def step(s, i):
                    for b, move in ((s + UNROLL, load), (s - LAG, store)):
                        if move is store and m == 1 and b >= MAX_BLOCKS:
                            continue
                        if 0 <= b < BLOCKS:
                            g = b // MAX_BLOCKS
                            move(g, b - g * MAX_BLOCKS + UNROLL * i, base + b, i)

                def steps(first, end):
                    for s in range(first, end):
                        step(s, ALONE)

                def loop(first, end):
                    with sp.Fori(0, (end - first) // UNROLL) as i:
                        for j in range(UNROLL):
                            step(first + j, i)

                sp.wait_ge(scattered[0], 16 * TOP * GT * (m + 1))
                for b in range(UNROLL):
                    load(0, b, base + b, ALONE)
                steps(0, HEAD)
                loop(HEAD, MAX_BLOCKS - UNROLL)
                sp.wait_ge(scattered[1], 16 * TOP * GT * (m + 1))
                steps(MAX_BLOCKS - UNROLL, MAX_BLOCKS + MIDDLE)
                loop(MAX_BLOCKS + MIDDLE, BLOCKS - UNROLL)
                steps(BLOCKS - UNROLL, BLOCKS + LAG)

            expert_phase(0)
            expert_phase(1)
            o_tiles = out.rearrange("b (t p) d -> p (b t) d", p=P)

            def store_out(t):
                sp.wait_ge(combined, TILES + t + 2)
                sp.dma_start(o_tiles[:, t:t + 2, :], xs[:, t:t + 2, :]).then_inc(out_stored, 16)

            for t in range(0, GT, 2):
                store_out(t)
            for k in range(UNROLL):
                stored = len([b for b in range(MAX_BLOCKS) if b % UNROLL == k])
                sp.wait_ge(final_stored[k], 16 * stored)
            final_tiles = final_rows[0:ROWS, :].rearrange("(p n) d -> p (n d)", p=P)
            for q in range(GT // 2):
                t = slice(2 * q, 2 * q + 2)
                part = slice(2 * q * TOP * D, 2 * (q + 1) * TOP * D)
                sp.dma_start(y_rows[1][:, t].rearrange("p t k d -> p (t k d)"),
                             final_tiles[:, part]).then_inc(final_loaded[q], 16)
            for t in range(GT, TILES, 2):
                store_out(t)
            sp.wait_ge(out_stored, 16 * TILES // 2)

        @block.gpsimd
        def _(pool):
            pool.memset(zeros[:], 0.0).then_inc(zeros_set, 1)
            pool.memset(ident[:], 0.0).then_inc(consts, 1)
            pool.memset(ident16[:], 0.0).then_inc(consts, 1)
            pool.memset(before16[:], 1.0).then_inc(consts, 1)
            pool.memset(ones16[:], 1.0).then_inc(consts, 1)
            pool.memset(causal16[:], 0.0).then_inc(consts, 1)
            pool.wait_ge(consts, 5)
            for m in (ident, ident16):
                pool.affine_select(out=m[:], in_=m[:], compare_op=ALU.not_equal, fill=1.0, base=0,
                                   pattern=[[-1, P]], channel_multiplier=1).then_inc(consts, 1)
            pool.affine_select(out=before16[:], in_=before16[:], compare_op=ALU.is_gt, fill=0.0, base=0,
                               pattern=[[1, P]], channel_multiplier=-1).then_inc(consts, 1)
            pool.affine_select(out=causal16[:], in_=causal16[:], compare_op=ALU.is_ge, fill=MASKED, base=0,
                               pattern=[[-1, P]], channel_multiplier=1).then_inc(consts, 1)
            pool.iota(rev_e[:], [[-1, E]], base=E, channel_multiplier=0,
                      allow_small_or_imprecise_dtypes=True).then_inc(consts, 1)
            pool.iota(block_floor[:], [[0, E], [P, GT]], base=0, channel_multiplier=0,
                      allow_small_or_imprecise_dtypes=True).then_inc(consts, 1)
            pool.iota(block_no[:], [[1, MAX_BLOCKS], [0, E - 1]], base=0, channel_multiplier=0,
                      allow_small_or_imprecise_dtypes=True).then_inc(consts, 1)
            for k in range(TOP):
                pool.iota(xn_numbered[k][:, :, D], [[TOP, GT]], base=k, channel_multiplier=TOP * GT,
                          allow_small_or_imprecise_dtypes=True).then_inc(consts, 1)
            pool.wait_ge(zeros_set, 1)
            for g in range(GROUPS):
                pool.dma_start(slots_in[g].rearrange("(p n) d -> p (n d)", p=P), zeros[:]).then_inc(slots_zeroed[g], 16)
            pool.memset(numbered[:], 0.0).then_inc(numbered_set, 1)
            pool.wait_ge(numbered_set, 1)
            pool.iota(numbered[:, :, D], [[1, MAX_BLOCKS]], base=ROWS, channel_multiplier=MAX_BLOCKS,
                      allow_small_or_imprecise_dtypes=True).then_inc(numbered_set, 1)

            def scatter(r):
                g = r % GROUPS
                if r < GROUPS:
                    pool.wait_ge(slots_zeroed[g], 16)
                pool.wait_ge(slotted, r + 1)
                for t in range(GT):
                    for k in range(TOP):
                        here, rows = slots_in[g], xn[g][:, t, :]
                        if r == 3:
                            here, rows = numbered_slots, xn_numbered[k][:, t, :]
                        pool.indirect_dma_start(
                            here, bass.IndirectOffsetOnAxis(ap=slot_of[g][:, k, t:t + 1], axis=0),
                            rows, None).then_inc(scattered[g], 16)

            def gather(p):
                g = p % GROUPS
                for k in range(UNROLL):
                    done = len([G for G in range((p + 1) * MAX_BLOCKS) if G % UNROLL == k])
                    pool.wait_ge(y_stored[k], 16 * done)
                for t in range(GT):
                    for k in range(TOP):
                        pool.indirect_dma_start(
                            y_rows[g][:, t, k, :], None, slots_out[g],
                            bass.IndirectOffsetOnAxis(ap=slot_of[g][:, k, t:t + 1], axis=0)
                        ).then_inc(gathered[g][t], 16)
                        yield

            def store_final(b):
                G = BLOCKS + MAX_BLOCKS + b
                pool.wait_ge(row_known, b + 1)
                pool.wait_ge(y_copied, G + 1)
                pool.indirect_dma_start(
                    final_rows, bass.IndirectOffsetOnAxis(ap=row_of[:, b:b + 1], axis=0),
                    yb[G % UNROLL][:], None).then_inc(final_stored[b % UNROLL], 16)

            scatter(0)
            scatter(1)
            pool.wait_ge(numbered_set, 2)
            pool.dma_start(numbered_slots.rearrange("(p n) d -> p n d", p=P), numbered[:]).then_inc(slots_numbered, 16)
            for p in range(GROUPS):
                for _ in gather(p):
                    pass
            scatter(2)
            pool.wait_ge(slots_numbered, 16)
            pool.wait_ge(second_copied, GT // 2)
            scatter(3)
            returning = gather(2)
            assert len([b for b in range(MAX_BLOCKS) if b % FINAL_PACE]) >= TOP * GT
            for b in range(MAX_BLOCKS):
                store_final(b)
                if b % FINAL_PACE:
                    next(returning, None)

        @block.scalar
        def _(sc):
            def copy_nT(n, h):
                g, idx = group_of_norm(n), 2 * n + h
                sc.wait_ge(nT_written, idx + 1)
                nc.scalar.copy(nT[g][:, h, :], nT_ps(n, h)[:]).then_inc(nT_copied, 1)

            def exp_logits(r):
                sc.wait_ge(shifted_ready, r + 1)
                nc.scalar.activation(expd[:], shifted[:], ACT.Exp).then_inc(expd_ready, 1)

            offset_regs = [sc.alloc_register(f"offset_act{n}") for n in range(UNROLL)]

            def expert_step(stages, c, s, i, offset):
                if 1 in stages:
                    G, k = nth(c - 1, i), (c - 1) % 2
                    if c - 1 >= 2:
                        sc.wait_ge(h_ready, G - 1)
                    nc.scalar.copy(w1_block[k][:], w1_sb[:, bass.ds(offset[s - 1], H)]).then_inc(w1_copied, 1)
                if 2 in stages:
                    G, k = nth(c - 2, i), (c - 2) % 2
                    sc.wait_ge(h_ready, G + 1)
                    if c - 2 >= 2:
                        sc.wait_ge(y_ready, G - 1)
                    nc.scalar.activation(act[k][:], h_ps[k][:], ACT.Gelu).then_inc(act_ready, 1)

            def expert_phase(m, **beside):
                sc.wait_ge(routed, GROUPS * m + 1)
                run_steps(sc, m, expert_step, table=(offset_regs, 1),
                          at_switch=lambda: sc.wait_ge(routed, GROUPS * (m + 1)), **beside)

            def project(a):
                for h in range(2):
                    sc.wait_ge(q_written[h], a + 1)
                    nc.scalar.copy(QT[h][:], q_ps[h][:]).then_inc(q_copied[h], 1)
                    sc.wait_ge(v_written[h], a + 1)
                    nc.scalar.copy(V[h][:].rearrange("p t d -> p (t d)"), v_ps[:]).then_inc(v_copied[h], 1)

            def attend(a):
                def soften(i, h):
                    n, t, w = HALF * a + i, GT * a + HALF * h + i, (i + 1) * P
                    sc.wait_ge(bias_ready[h], n + 1)
                    if n >= 2:
                        sc.wait_ge(pT_written[h], n - 1)
                    nc.scalar.activation(probs[h][n % 2][:, 0:w], s_ps[h][n % 2][:, 0:w], ACT.Exp,
                                         bias=exp_bias[:, t:t + 1], scale=SCORE_SCALE,
                                         accum_out=row_sum[:, t:t + 1]).then_inc(exped[h], 1)

                def copy_pT(i, h):
                    n, w = HALF * a + i, (i + 1) * P
                    sc.wait_ge(pT_written[h], n + 1)
                    if n:
                        sc.wait_ge(o_written[h], n)
                    nc.scalar.copy(probs_T[h][:, 0:w], pT_ps[h][:, 0:w]).then_inc(pT_copied[h], 1)

                units = [(i, h) for i in range(HALF) for h in range(2)]
                soften(*units[0])
                soften(*units[1])
                for u in range(GT):
                    if u + 2 < GT:
                        soften(*units[u + 2])
                    copy_pT(*units[u])

            def copy_both(n):
                copy_nT(n, 0)
                copy_nT(n, 1)

            sc.wait_ge(router_T_ps, 1)
            nc.scalar.copy(router_T[:], router_ps[:, 0:E]).then_inc(router_T_sb, 1)
            copy_both(NORM_OF_ROUTE[0])
            exp_logits(0)
            copy_both(NORM_OF_ROUTE[1])
            exp_logits(1)
            sc.wait_ge(w1_in, 16 * E // 2)
            expert_phase(0)
            copy_both(NORM_OF_ATTEND[0])
            project(0)
            attend(0)
            copy_both(NORM_OF_ROUTE[2])
            exp_logits(2)
            copy_both(NORM_OF_ATTEND[1])
            project(1)
            attend(1)

            def route_last(s):
                if s == TRANSPOSES_BESIDE:
                    copy_nT(NORM_OF_ROUTE[3], 0)
                if s == TRANSPOSES_BESIDE + 1:
                    copy_nT(NORM_OF_ROUTE[3], 1)
                q = s - TRANSPOSES_BESIDE - 2
                if 0 <= q < GT // 2:
                    pair_of_tiles = slice(2 * q, 2 * q + 2)
                    nc.scalar.copy(xn_numbered[1][:, pair_of_tiles, 0:D],
                                   xn[1][:, pair_of_tiles, :]).then_inc(second_copied, 1)

            expert_phase(1, head=LONG_HEAD, beside=route_last)
            exp_logits(3)

        @block.vector
        def _(dve):
            v = nc.vector
            steps = [0]
            counts = [0]
            unaggregated = []

            def then(ins):
                ins.then_inc(dve_step, 1)
                steps[0] += 1
                dve.wait_ge(dve_step, steps[0])
                return ins

            def aggregate():
                if unaggregated:
                    t, count = unaggregated.pop()
                    dve.wait_ge(counted, count)
                    return v.bn_aggr(moments[:, t, :], stats[t // GT][:, t % GT, :])

            def tile_stats(t):
                v.bn_stats(stats[t // GT][:, t % GT, :], xs[:, t, :]).then_inc(counted, 1)
                counts[0] += 1
                aggregate()
                unaggregated.append((t, counts[0]))

            ln_work = var_eps, half_bits, rstd, newton


            def normalise(*norms):
                tiles = [(n, t) for n in norms for t in range(GT)]
                then(aggregate())
                first = GT * group_of_norm(norms[0])
                var_eps, half_bits, rstd, newton = (a[:, first:first + len(tiles)] for a in ln_work)
                then(v.tensor_scalar(var_eps, moments[:, first:first + len(tiles), 1], LN_EPS, None, ALU.add))
                then(v.tensor_scalar(half_bits, var_eps.bitcast(I32), 1, None, ALU.logical_shift_right))
                then(v.tensor_scalar(rstd.bitcast(I32), half_bits, -1.0, RSQRT_MAGIC, ALU.mult, ALU.add))
                yield
                for k in range(NEWTON_STEPS):
                    if k == 2:
                        yield
                    then(v.tensor_tensor(newton, rstd, rstd, ALU.mult))
                    then(v.scalar_tensor_tensor(newton, newton, -0.5, var_eps, ALU.mult, ALU.mult))
                    then(v.scalar_tensor_tensor(rstd, newton, 1.5, rstd, ALU.add, ALU.mult))
                for j, (n, t) in enumerate(tiles):
                    if j and j % HALF == 0:
                        yield
                    g = group_of_norm(n)
                    v.tensor_scalar(xn[g][:, t, :], xs[:, g * GT + t, :], moments[:, g * GT + t, 0:1], rstd[:, j:j + 1],
                                    ALU.subtract, ALU.mult).then_inc(normed, 1)
                dve.wait_ge(normed, (norms[-1] + 1) * GT)
                yield

            def per_tile(a):
                return a[:].unsqueeze(2).to_broadcast([P, GT, E])

            def pick_top(scores, chosen):
                then(v.tensor_tensor(key[:], scores[:], per_tile(top), ALU.is_equal))
                then(v.tensor_tensor(key[:], key[:], rev_e[:].unsqueeze(1).to_broadcast([P, GT, E]), ALU.mult))
                then(v.tensor_reduce(best[:], key[:], AX, ALU.max))
                then(v.tensor_tensor(chosen[:], key[:], per_tile(best), ALU.is_equal))

            def route(r):
                g = r % GROUPS
                dve.wait_ge(logits_ready, r + 1)
                then(v.tensor_copy(logit[:], logit_ps.rearrange("p (t e) -> p t e", e=E)))
                then(v.tensor_reduce(top[:], logit[:], AX, ALU.max))
                v.tensor_tensor(shifted[:], logit[:], per_tile(top), ALU.subtract).then_inc(shifted_ready, 1)
                yield
                pick_top(logit, pick1)
                dve.wait_ge(shifted_ready, r + 1)
                yield
                then(v.scalar_tensor_tensor(logit2[:], pick1[:], MASKED, logit[:], ALU.mult, ALU.add))
                then(v.tensor_reduce(top[:], logit2[:], AX, ALU.max))
                pick_top(logit2, pick2)
                v.tensor_tensor(picked16[:], pick1[:], pick2[:], ALU.add).then_inc(picked_ready, 1)
                yield
                dve.wait_ge(ranked, r + 1)
                then(v.tensor_tensor(over[:], count_ps.unsqueeze(2).to_broadcast([P, E, GT]),
                                     block_floor[:], ALU.is_gt))
                then(v.tensor_reduce(n_blocks[:], over[:], AX, ALU.add))
                then(v.tensor_tensor_scan(last_block[:], n_blocks[:], n_blocks[:], 0.0, ALU.add, ALU.bypass))
                then(v.tensor_tensor(first_block[:], last_block[:], n_blocks[:], ALU.subtract))
                then(v.scalar_tensor_tensor(
                    slot[:], first_block[:].unsqueeze(1).to_broadcast([P, GT, E]), float(P),
                    rank_ps.rearrange("p (t e) -> p t e", e=E), ALU.mult, ALU.add))
                yield
                for k, chosen in enumerate((pick1, pick2)):
                    then(v.tensor_tensor(work[:], slot[:], chosen[:], ALU.mult))
                    then(v.tensor_reduce(slot_f[:, k, :], work[:], AX, ALU.add))
                v.tensor_copy(slot_of[g][:], slot_f[:]).then_inc(slotted, 1)
                yield
                then(v.tensor_tensor(past[:], block_no[:],
                                     last_block[0:1, 0:E - 1].unsqueeze(1).to_broadcast([1, MAX_BLOCKS, E - 1]),
                                     ALU.is_ge))
                then(v.tensor_reduce(expert_f[:], past[:], AX, ALU.add))
                v.tensor_scalar(expert_at[:, g * MAX_BLOCKS:(g + 1) * MAX_BLOCKS], expert_f[:], float(H), None,
                                ALU.mult).then_inc(routed, 1)
                dve.wait_ge(routed, r + 1)
                yield

            def gates(r):
                g = r % GROUPS
                dve.wait_ge(expd_ready, r + 1)
                then(v.tensor_reduce(den[:], expd[:], AX, ALU.add))
                then(v.reciprocal(prob1[:], den[:]))
                then(v.tensor_tensor(work[:], expd[:], pick2[:], ALU.mult))
                then(v.tensor_reduce(prob2[:], work[:], AX, ALU.add))
                yield
                then(v.tensor_tensor(prob2[:], prob2[:], prob1[:], ALU.mult))
                then(v.scalar_tensor_tensor(den[:], prob1[:], TOPK_EPS, prob2[:], ALU.add, ALU.add))
                then(v.reciprocal(den[:], den[:]))
                then(v.scalar_tensor_tensor(gate[g][:, 0, :], prob1[:], 0.5, den[:], ALU.mult, ALU.mult))
                then(v.scalar_tensor_tensor(gate[g][:, 1, :], prob2[:], 0.5, den[:], ALU.mult, ALU.mult))
                yield

            def rest(pieces):
                for _ in pieces:
                    pass

            def expert_step(stages, c, s, i):
                m = (c - s) // BLOCKS
                if 0 in stages:
                    G, k = nth(c, i), c % UNROLL
                    dve.wait_ge(xT_ready, G + 1)
                    if c >= UNROLL:
                        dve.wait_ge(h_ready, G - UNROLL + 1)
                    v.tensor_copy(xT[k][:], xT_ps[c % 2][:, 0:P]).then_inc(xT_copied, 1)
                    b = s - MAX_BLOCKS
                    if m == 1 and b >= 0:
                        v.tensor_copy(row_of[:, b:b + 1], xb_numbered[k][:, D:D + 1]).then_inc(row_known, 1)
                if 3 in stages:
                    c3 = c - 3
                    G, k = nth(c3, i), c3 % UNROLL
                    dve.wait_ge(y_ready, G + 1)
                    b = s - LAG - MAX_BLOCKS
                    if m == 1 and b >= UNROLL:
                        dve.wait_ge(final_stored[b % UNROLL], 16 * (b // UNROLL + i))
                    elif c3 >= UNROLL:
                        dve.wait_ge(y_stored[k], 16 * (uses(c3, i) - 1))
                    v.tensor_copy(yb[k][:], y_ps[c3 % 2][:, 0:D]).then_inc(y_copied, 1)

            def combine(p, tiles):
                g = p % GROUPS
                for k in range(TOP):
                    for n, t in enumerate(tiles):
                        tile = xs[:, g * GT + t, :]
                        if k:
                            dve.wait_ge(dve_step, steps[0] - len(tiles) + n + 1)
                        elif p == 3:
                            dve.wait_ge(final_loaded[t // 2], 16)
                        else:
                            dve.wait_ge(gathered[g][t], 16 * TOP * (p // GROUPS + 1))
                        add = v.scalar_tensor_tensor(tile, y_rows[g][:, t, k, :], gate[g][:, k, t:t + 1], tile,
                                                     ALU.mult, ALU.add)
                        add.then_inc(combined if k else dve_step, 1)
                    if not k:
                        steps[0] += len(tiles)

            def combine_and_count(p, tiles):
                combine(p, tiles)
                for t in tiles:
                    dve.wait_ge(combined, p * GT + t + 1)
                    tile_stats(p * GT + t)

            def pair_of(q):
                return range(2 * q, 2 * q + 2)

            def copy_keys(a):
                for h in range(2):
                    dve.wait_ge(k_written[h], a + 1)
                    v.tensor_copy(KT[h][:], k_ps[h][:]).then_inc(k_copied[h], 1)

            def attend(a, beside):
                def maxima(i, h):
                    n, t, w = HALF * a + i, GT * a + HALF * h + i, (i + 1) * P
                    dve.wait_ge(scored[h], n + 1)
                    then(v.reduce_max(neg_max[:, t:t + 1], s_ps[h][n % 2][:, 0:w], AX, negate=True))
                    v.tensor_scalar(exp_bias[:, t:t + 1], neg_max[:, t:t + 1], SCORE_SCALE, None,
                                    ALU.mult).then_inc(bias_ready[h], 1)

                def finish(i, h):
                    n, t = HALF * a + i, GT * a + HALF * h + i
                    dve.wait_ge(exped[h], n + 1)
                    then(v.reciprocal(row_inv[:, t:t + 1], row_sum[:, t:t + 1]))
                    dve.wait_ge(o_written[h], n + 1)
                    v.scalar_tensor_tensor(xs[:, t, :], o_ps[h][:, 0:D], row_inv[:, t:t + 1],
                                           xs[:, t, :], ALU.mult, ALU.add).then_inc(attended[h], 1)
                    beside(2 * i + h)
                    dve.wait_ge(attended[h], n + 1)
                    tile_stats(t)

                units = [(i, h) for i in range(HALF) for h in range(2)]
                for u in range(3):
                    maxima(*units[u])
                for u in range(GT):
                    if u + 3 < GT:
                        maxima(*units[u + 3])
                    finish(*units[u])

            dve.wait_ge(consts, 14)
            for t in range(GT):
                if t % HALF == 0:
                    dve.wait_ge(x_in[0][t // HALF], 16)
                tile_stats(t)
            rest(normalise(NORM_OF_ROUTE[0]))
            rest(route(0))
            rest(gates(0))
            for t in range(GT):
                if t % HALF == 0:
                    dve.wait_ge(x_in[1][t // HALF], 16)
                tile_stats(GT + t)
            rest(normalise(NORM_OF_ROUTE[1]))
            pieces = chain(route(1), gates(1))

            next(pieces)
            next(pieces)

            def beside_first(s):
                q, odd = divmod(s - FIRST_COMBINE, 2)
                if s < MAX_BLOCKS:
                    next(pieces, None)
                elif s == MAX_BLOCKS:
                    rest(pieces)
                    dve.wait_ge(scattered[0], 16 * TOP * GT)
                elif q >= GT // 2:
                    next(norm_pieces, None)
                elif q >= 0 and odd:
                    combine_and_count(0, pair_of(q))

            norm_pieces = normalise(NORM_OF_ATTEND[0])
            run_steps(dve, 0, expert_step, head=LONG_HEAD, middle=MAX_BLOCKS, beside=beside_first)
            rest(norm_pieces)
            copy_keys(0)
            attend(0, lambda u: combine_and_count(1, pair_of(u // 2 - 1)) if u in (2, 4, 6) else None)
            combine_and_count(1, pair_of(3))
            dve.wait_ge(scattered[1], 16 * TOP * GT)
            rest(normalise(NORM_OF_ROUTE[2], NORM_OF_ATTEND[1]))
            rest(route(2))
            copy_keys(1)
            attend(1, lambda u: None)
            pieces = chain(normalise(NORM_OF_ROUTE[3]), gates(2), iter([None]), route(3))
            for _ in range(3):
                next(pieces)

            def beside_last(s):
                q, r = divmod(s - (MAX_BLOCKS + LAG - 2) - 2 * FINAL_PACE, FINAL_PACE)
                if s < MAX_BLOCKS:
                    next(pieces, None)
                elif 0 <= q < GT // 2 and r == 0:
                    combine(2, pair_of(q))
                    combined_pairs.append(q)

            combined_pairs = []
            run_steps(dve, 1, expert_step, head=LONG_HEAD, middle=MAX_BLOCKS, beside=beside_last)
            rest(gates(3))
            combine(2, range(2 * len(combined_pairs), GT))
            for q in range(GT // 2):
                combine(3, pair_of(q))

        @block.tensor
        def _(pe):
            offset_regs = [pe.alloc_register(f"offset_pe{n}") for n in range(UNROLL)]

            def transpose_normed(n, h):
                g, idx = group_of_norm(n), 2 * n + h
                if idx >= 2:
                    pe.wait_ge(nT_copied, idx - 1)
                if n == NORM_OF_ROUTE[3] and h:
                    pe.wait_ge(nT_copied, idx)
                for t in range(HALF):
                    pe.wait_ge(normed, n * GT + h * HALF + t + 1)
                    mm = nc.tensor.transpose(nT_ps(n, h)[:, t * P:(t + 1) * P], xn[g][:, h * HALF + t, :], ident[:])
                mm.then_inc(nT_written, 1)

            def transpose_both(n):
                transpose_normed(n, 0)
                transpose_normed(n, 1)

            def logits(r):
                g, n = r % GROUPS, NORM_OF_ROUTE[r]
                if r:
                    pe.wait_ge(routed, r)
                for h in range(2):
                    pe.wait_ge(nT_copied, 2 * n + h + 1)
                    for t in range(HALF):
                        c = (h * HALF + t) * E
                        mm = nc.tensor.matmul(logit_ps[:, c:c + E], nT[g][:, h, t * P:(t + 1) * P], router_T[:],
                                              start=True, stop=True)
                mm.then_inc(logits_ready, 1)

            def ranks(r):
                pe.wait_ge(picked_ready, r + 1)
                flat = picked16[:].rearrange("p t e -> p (t e)")
                nc.tensor.matmul(rank_ps, before16[:], flat, start=True, stop=True, skip_group_check=True)
                for k in range(1, GT):
                    nc.tensor.matmul(rank_ps[:, k * E:GT * E], ones16[:], flat[:, 0:(GT - k) * E],
                                     start=False, stop=True, skip_group_check=True)
                for t in range(GT):
                    mm = nc.tensor.matmul(count_ps, ones16[:], picked16[:, t, :], start=(t == 0), stop=(t == GT - 1))
                mm.then_inc(ranked, 1)

            def expert_phase(m, **beside):
                def step(stages, c, s, i, offset):
                    if 0 in stages:
                        G, k = nth(c, i), c % 2
                        pe.wait_ge(x_loaded[c % UNROLL], 16 * uses(c, i))
                        if c >= 2:
                            pe.wait_ge(xT_copied, G - 1)
                        nc.tensor.transpose(xT_ps[k][:, 0:P], xb[c % UNROLL][:], ident[:]).then_inc(xT_ready, 1)
                    if 2 in stages:
                        c2 = c - 2
                        G, k = nth(c2, i), c2 % 2
                        pe.wait_ge(xT_copied, G + 1)
                        pe.wait_ge(w1_copied, G + 1)
                        if c2 >= 2:
                            pe.wait_ge(act_ready, G - 1)
                        for q in range(HC):
                            mm = nc.tensor.matmul(h_ps[k][:, q * P:(q + 1) * P], w1_block[k][:, q * P:(q + 1) * P],
                                                  xT[c2 % UNROLL][:], start=True, stop=True)
                        mm.then_inc(h_ready, 1)
                    if 3 in stages:
                        c3 = c - 3
                        G, k = nth(c3, i), c3 % 2
                        at = offset[s - 3]
                        pe.wait_ge(act_ready, G + 1)
                        if c3 >= 2:
                            pe.wait_ge(y_copied, G - 1)
                        for q in range(HC):
                            mm = nc.tensor.matmul(y_ps[k][:, 0:D], act[k][:, q * P:(q + 1) * P],
                                                  w2_sb[:, bass.ds(at + q * D, D)], start=(q == 0), stop=(q == HC - 1))
                        mm.then_inc(y_ready, 1)

                pe.wait_ge(routed, GROUPS * m + 1)
                run_steps(pe, m, step, table=(offset_regs, LAG),
                          at_switch=lambda: pe.wait_ge(routed, GROUPS * (m + 1)), **beside)

            def project(a, h, between=lambda: None):
                pe.wait_ge(nT_copied, 2 * NORM_OF_ATTEND[a] + h + 1)
                x_T = nT[a][:, h, :]
                nc.tensor.matmul(q_ps[h][:], qw[:], x_T, start=True, stop=True).then_inc(q_written[h], 1)
                nc.tensor.matmul(k_ps[h][:], kw[:], x_T, start=True, stop=True).then_inc(k_written[h], 1)
                between()
                if h:
                    pe.wait_ge(v_copied[0], a + 1)
                for t in range(HALF):
                    mm = nc.tensor.matmul(v_ps[:, t * D:(t + 1) * D], x_T[:, t * P:(t + 1) * P], vw[:],
                                          start=True, stop=True)
                mm.then_inc(v_written[h], 1)

            def attend(a):
                def score(i, h):
                    n, w = HALF * a + i, (i + 1) * P
                    if i >= 2:
                        pe.wait_ge(exped[h], n - 1)
                    bank_s = s_ps[h][n % 2]
                    nc.tensor.matmul(bank_s[:, 0:w], QT[h][:, i * P:w], KT[h][:, 0:w], start=True, stop=True,
                                     skip_group_check=True)
                    nc.tensor.matmul(bank_s[:, i * P:w], ident16[:], causal16[:], start=False, stop=True,
                                     skip_group_check=True).then_inc(scored[h], 1)

                def transpose_probs(i, h):
                    n = HALF * a + i
                    pe.wait_ge(exped[h], n + 1)
                    if i:
                        pe.wait_ge(pT_copied[h], n)
                    for j in range(i + 1):
                        mm = nc.tensor.transpose(pT_ps[h][:, j * P:(j + 1) * P],
                                                 probs[h][n % 2][:, j * P:(j + 1) * P], ident[:])
                    mm.then_inc(pT_written[h], 1)

                def mix(i, h):
                    n = HALF * a + i
                    pe.wait_ge(pT_copied[h], n + 1)
                    if i:
                        pe.wait_ge(attended[h], n)
                    for j in range(i + 1):
                        mm = nc.tensor.matmul(o_ps[h][:, 0:D], probs_T[h][:, j * P:(j + 1) * P], V[h][:, j, :],
                                              start=(j == 0), stop=(j == i))
                    mm.then_inc(o_written[h], 1)

                for h in range(2):
                    pe.wait_ge(q_copied[h], a + 1)
                    pe.wait_ge(k_copied[h], a + 1)
                pe.wait_ge(v_copied[1], a + 1)
                units = [(i, h) for i in range(HALF) for h in range(2)]
                for u in range(3):
                    score(*units[u])
                transpose_probs(*units[0])
                for u in range(GT):
                    if u + 3 < GT:
                        score(*units[u + 3])
                    if u + 1 < GT:
                        transpose_probs(*units[u + 1])
                    mix(*units[u])

            pe.wait_ge(consts, 14)
            pe.wait_ge(router_in, 16)
            nc.tensor.transpose(router_ps[:, 0:E], router_rows[:], ident[0:E, 0:E]).then_inc(router_T_ps, 1)
            pe.wait_ge(router_T_sb, 1)
            transpose_both(NORM_OF_ROUTE[0])
            logits(0)
            ranks(0)
            transpose_both(NORM_OF_ROUTE[1])
            logits(1)
            pe.wait_ge(w2_in, 16 * E // 2)
            expert_phase(0, beside=lambda s: ranks(1) if s == FIRST_RANKS_BESIDE else None)
            pe.wait_ge(y_copied, BLOCKS)
            pe.wait_ge(attn_w_in, 48)
            transpose_both(NORM_OF_ATTEND[0])
            project(0, 0)
            project(0, 1)
            attend(0)
            for h in range(2):
                pe.wait_ge(attended[h], HALF)
            transpose_both(NORM_OF_ROUTE[2])
            logits(2)
            transpose_both(NORM_OF_ATTEND[1])
            project(1, 0, between=lambda: ranks(2))
            project(1, 1)
            pe.wait_ge(routed, 3)
            attend(1)
            for h in range(2):
                pe.wait_ge(attended[h], 2 * HALF)

            def route_last(s):
                if s == TRANSPOSES_BESIDE:
                    transpose_normed(NORM_OF_ROUTE[3], 0)
                if s == TRANSPOSES_BESIDE + 1:
                    transpose_normed(NORM_OF_ROUTE[3], 1)
                if s == LOGITS_BESIDE:
                    logits(3)
                if s == RANKS_BESIDE:
                    ranks(3)

            expert_phase(1, head=LONG_HEAD, beside=route_last)


_INS = ['L0_attn_x', 'L0_attn_Qw', 'L0_attn_Kw', 'L0_attn_Vw', 'L0_ffn_router_w', 'L0_ffn_w1', 'L0_ffn_w2']


def kernel(**inputs):
    import numpy as _np
    import concourse.bacc as _bacc
    from concourse import mybir as _mybir
    from concourse.bass_utils import run_bass_kernel_spmd as _run

    nc = _bacc.Bacc("TRN2", target_bir_lowering=False, num_devices=1)
    arrays, args = {}, []
    for name in _INS:
        a = _np.ascontiguousarray(inputs[name])
        arrays[f"in_{name}"] = a
        args.append(nc.dram_tensor(f"in_{name}", a.shape, _mybir.dt.from_np(a.dtype), kind="ExternalInput").ap())
    out = nc.dram_tensor("out", inputs['L0_attn_x'].shape, _mybir.dt.float32, kind="ExternalOutput").ap()
    macaron(nc, *args, out)
    r = _run(nc, [arrays], core_ids=[0])
    return r.results[0]["out"]
```
